# Optimizing a Trainium2 kernel written in Bass

```python
import numpy as np
import jax
import jax.numpy as jnp

def _softmax(x, axis=-1):
    return jax.nn.softmax(x, axis=axis)

def _gelu(x):
    return jax.nn.gelu(x, approximate=True)

def _silu(x):
    return jax.nn.silu(x)

def _sigmoid(x):
    return jax.nn.sigmoid(x)

def _layernorm(x, axis=-1, eps=1e-05):
    m = jnp.mean(x, axis=axis, keepdims=True)
    v = jnp.var(x, axis=axis, keepdims=True)
    return (x - m) / jnp.sqrt(v + eps)

def _scatter_add(tgt, idx, src, axis=0):
    return tgt.at[idx].add(src)

def _segment_sum(src, seg, n):
    return jax.ops.segment_sum(src, seg, n)
kernel_name = 'mk_adj_resnorm_d1_adj_r2_4e70a7'

def setup_inputs(seed: int=0):
    np.random.seed(seed)
    _w = jnp.asarray

    def _rec_inputs():
        import jax
        import jax.numpy as jnp
        _gk = jax.random.key(seed)
        x = -9.806e-05 + 1 * jax.random.normal(jax.random.fold_in(_gk, 1), (8192, 128), jnp.float32)
        _a = jax.random.bernoulli(jax.random.fold_in(_gk, 2), 0.00195312, (8192, 8192))
        _a = jnp.logical_or(_a, jnp.eye(8192, dtype=bool))
        _af = _a.astype(jnp.float32)
        _af = _af * jax.random.uniform(jax.random.fold_in(_gk, 3), (8192, 8192), jnp.float32, 0.05, 1)
        adj = _af
        return (x, adj)
    x, adj = _rec_inputs()

    def _L0_gnn_setup():
        import jax, jax.numpy as jnp
        import numpy as np

        def _lap_mul(A, x):
            d = 1.0 / jnp.sqrt(jnp.sum(A, axis=-1))
            return d[:, None] * (A @ (d[:, None] * x))
        key = jax.random.key(seed)
        k1, k2, k3, k4, k5, k6 = jax.random.split(key, 6)
        N, D_IN, D_OUT = (2048, 128, 128)
        x = jax.random.normal(k1, (N, D_IN), dtype=jnp.float32)
        A = jax.random.uniform(k2, (N, N), dtype=jnp.float32)
        s1 = 1.0 / np.sqrt(D_IN)
        W1 = jax.random.uniform(k3, (D_IN, D_OUT), minval=-s1, maxval=s1, dtype=jnp.float32)
        b1 = jax.random.uniform(k4, (D_OUT,), minval=-s1, maxval=s1, dtype=jnp.float32)
        W2 = jax.random.uniform(k5, (D_IN, D_OUT), minval=-s1, maxval=s1, dtype=jnp.float32)
        b2 = jax.random.uniform(k6, (D_OUT,), minval=-s1, maxval=s1, dtype=jnp.float32)
        return {'x': x, 'A': A, 'W1': W1, 'b1': b1, 'W2': W2, 'b2': b2, 'sigma': 1, 'k': 4}
    _L0_gnn_all = _L0_gnn_setup()
    _L0_gnn_in = {k: v for k, v in _L0_gnn_all.items() if k in ('W1', 'b1', 'W2', 'b2')}
    del _L0_gnn_all
    return {'x': x, 'adj': adj, 'L0_gnn_W1': _L0_gnn_in['W1'], 'L0_gnn_b1': _L0_gnn_in['b1'], 'L0_gnn_W2': _L0_gnn_in['W2'], 'L0_gnn_b2': _L0_gnn_in['b2']}

def reference(x, adj, L0_gnn_W1, L0_gnn_b1, L0_gnn_W2, L0_gnn_b2):
    import jax
    import jax.numpy as jnp

    def _L0_gnn_ref(x, A, W1, b1, W2, b2, sigma, k):
        import jax, jax.numpy as jnp
        import numpy as np

        def _lap_mul(A, x):
            d = 1.0 / jnp.sqrt(jnp.sum(A, axis=-1))
            return d[:, None] * (A @ (d[:, None] * x))
        z = _lap_mul(A, x) @ W1 + b1
        z = jax.nn.leaky_relu(z, negative_slope=0.1)
        sq = jnp.sum(z * z, axis=-1)
        d2 = sq[:, None] + sq[None, :] - 2.0 * (z @ z.T)
        d2 = jnp.maximum(d2, 0.0)
        S = jnp.sqrt(d2 + 1e-10)
        S = jnp.exp(-S / (2.0 * sigma))
        order = jnp.argsort(-S, axis=-1)
        ranks = jnp.argsort(order, axis=-1)
        S = jnp.where(ranks < k, S, 0.0)
        A2 = S + A
        out = _lap_mul(A2, x) @ W2 + b2
        return out
    x = _layernorm(x + _L0_gnn_ref(x, adj, L0_gnn_W1, L0_gnn_b1, L0_gnn_W2, L0_gnn_b2, 1, 4), axis=-1)
    return x

_drawn_inputs = setup_inputs


def setup_inputs(seed=0):
    import zlib

    import numpy as np

    out = dict(_drawn_inputs(seed))
    spreads = {}
    factors = {}
    for name, (base, spread) in spreads.items():
        noise = np.random.default_rng([zlib.crc32(name.encode()), seed]).standard_normal(out[name].shape)
        drawn = base * np.exp(spread * noise) if base else spread * noise
        out[name] = jnp.asarray(drawn.astype(out[name].dtype))
    for name, factor in factors.items():
        out[name] = (out[name] * factor).astype(out[name].dtype)
    return out
```

```python
from contextlib import ExitStack

import concourse.bass as bass
from concourse import mybir

F32 = mybir.dt.float32
F32R = mybir.dt.float32r
BF16 = mybir.dt.bfloat16
U32 = mybir.dt.uint32
I32 = mybir.dt.int32
ALU = mybir.AluOpType
ACT = mybir.ActivationFunctionType
AX_X = mybir.AxisListType.X

P = 128
BLK = 512
TPB = BLK // P
GT = 8
KNN = 4
TOP = 8
LAG = 2
EPS_D2 = 1e-10
EPS_LN = 1e-5
ds = bass.ds


def gnn_resnorm(nc, x, xT, adjb, W1, b1, W2, b2, out):
    N, D = x.shape
    NT = N // P
    NB = N // BLK
    NG = NT // GT
    BPG = GT // TPB
    IBS = NB // GT
    QW = 2048
    NQ = N // QW
    HW = 2 * BLK
    NH = N // HW
    NC = NQ * TOP
    R2 = 6
    WB = TPB * BLK
    assert D == P and IBS == 2 and NB == 16 and NG > LAG + 1

    x_t = x.rearrange("(t p) f -> p t f", p=P)
    out_t = out.rearrange("(t p) f -> p t f", p=P)
    yw_table = nc.dram_tensor("yw_table", (N, D), F32, kind="Internal").ap()
    yw_t = yw_table.rearrange("(t p) f -> p t f", p=P)

    whole = ExitStack()
    with whole:
        def maker(stack):
            return lambda name, shape, dt=F32, side=None: stack.enter_context(
                nc.sbuf_tensor(name, shape, dt, **({"side": side} if side else {})))

        def sem(name):
            return whole.enter_context(nc.semaphore(name))

        def psum(name, shape):
            return whole.enter_context(nc.psum_tensor(name, shape, F32))

        sb = maker(whole)
        aggT = sb("aggT", [P, N])
        y1 = sb("y1", [P, NT * D])
        w1 = sb("w1", [P, D])
        w2 = sb("w2", [P, D])
        b1b = sb("b1b", [P, D])
        b2b = sb("b2b", [P, D])
        ident = sb("ident", [P, P])
        identb = sb("identb", [P, P], BF16)
        onesb = sb("onesb", [P, P], BF16)
        ones = sb("ones", [P, 1])
        half = sb("half", [P, GT * KNN])
        neghalf = sb("neghalf", [P, GT])
        iota_i = sb("iota_i", [P, 2 * NC], I32)
        iota_c = sb("iota_c", [P, NC])
        quarter_at = sb("quarter_at", [P, NC])
        rs_all = sb("rs_all", [P, NT])
        d1_all = sb("d1_all", [P, NT])
        d2_all = sb("d2_all", [P, NT])
        sq_all = sb("sq_all", [P, NT])
        s_all = sb("s_all", [P, NT * KNN])
        nb_all = sb("nb_all", [P, NT * KNN], U32)
        rs_c = sb("rs_c", [P, TPB])
        d1_c = sb("d1_c", [P, TPB])

        gb = psum("gb", [P, 4, BLK])
        pp = psum("pp", [P, 2, BLK])
        px = psum("px", [P, 2, BLK])
        ps_rs, ps_z, ps_zt, ps_sq = (gb[:, k, :] for k in range(4))

        consts_loaded = sem("consts_loaded")
        pool_consts = sem("pool_consts")
        wait_carrier = sem("wait_carrier")
        agg_zeroed = sem("agg_zeroed")
        loaded = [sem(f"loaded{k}") for k in range(NB)]
        rows_added = sem("rows_added")
        p1_rows = sem("p1_rows")
        p1_tail = sem("p1_tail")
        rowsum_ready = sem("rowsum_ready")
        rs_ready = sem("rs_ready")
        d1_ready = sem("d1_ready")
        d1_stored = sem("d1_stored")
        y1_ready = sem("y1_ready")
        agg_saved = sem("agg_saved")
        p2_blocks = sem("p2_blocks")
        p2_rows = sem("p2_rows")
        usum_ready = sem("usum_ready")
        z_ready = sem("z_ready")
        zstep = sem("zstep")
        z_done = sem("z_done")
        zt_ready = sem("zt_ready")
        zh_done = sem("zh_done")
        zl_done = sem("zl_done")
        sqrow_zeroed = sem("sqrow_zeroed")
        sqrow_done = sem("sqrow_done")
        stat_ready = sem("stat_ready")
        gram_free = sem("gram_free")
        gram_ready = sem("gram_ready")
        quarter_ready = sem("quarter_ready")
        quarter_free = sem("quarter_free")
        knn_step = sem("knn_step")
        grp_step = sem("grp_step")
        v_ready = sem("v_ready")
        r_ready = sem("r_ready")
        s_ready = sem("s_ready")
        pool_step = sem("pool_step")
        ystage_ready = sem("ystage_ready")
        ycur_ready = sem("ycur_ready")
        nb_ready = sem("nb_ready")
        xg_loaded = sem("xg_loaded")
        xtg_loaded = sem("xtg_loaded")
        psx_ready = sem("psx_ready")
        yw_done = sem("yw_done")
        yw_stored = sem("yw_stored")
        a_loaded = [sem(f"a_loaded{k}") for k in range(IBS)]
        prod_ready = sem("prod_ready")
        prod_free = sem("prod_free")
        idx_ready = sem("idx_ready")
        gathered = [sem(f"gathered{k}") for k in range(2)]
        scal_ready = sem("scal_ready")
        gs_step = sem("gs_step")
        gsum_done = sem("gsum_done")
        ofin_ready = sem("ofin_ready")
        fin_ready = sem("fin_ready")
        fin_step = sem("fin_step")
        norm_step = sem("norm_step")
        xb_loaded = [sem(f"xb_loaded{k}") for k in range(2)]
        var_ready = sem("var_ready")
        sd_ready = sem("sd_ready")
        y_ready = sem("y_ready")
        y_stored = [sem(f"y_stored{k}") for k in range(2)]

        scope = ExitStack()
        s1 = maker(scope)
        ring1 = s1("ring1", [P, NB, WB])
        acc = s1("acc", [P, WB])
        scope.close()

        right = ExitStack()
        sr = maker(right)
        zTh = sr("zTh", [P, N], F32R, "right")
        zTl = sr("zTl", [P, N], F32R, "right")
        sqrow = sr("sqrow", [P, N], BF16, "right")
        scope = ExitStack()
        s2 = maker(scope)
        ring2 = s2("ring2", [P, R2, WB])
        usum = s2("usum", [P, BLK])
        z_c = s2("z_c", [P, TPB, D])
        junk = s2("junk", [P, TPB, D])
        d1_z = s2("d1_z", [P, TPB])
        sq_c = s2("sq_c", [P, TPB])
        sq_r = s2("sq_r", [P, TPB])
        sq_parts = s2("sq_parts", [P, TPB, 3], BF16)
        scope.close()

        scope = ExitStack()
        s3 = maker(scope)
        keys = y1[:, :].rearrange("p (s w) -> p s w", w=QW)
        a_ring = s3("a_ring", [P, IBS, BPG * WB])
        ycur = s3("ycur", [P, GT * D])
        ystage = s3("ystage", [P, GT, D])
        x_g = s3("x_g", [P, GT, D])
        xw_g = s3("xw_g", [P, GT * D])
        stat_h = s3("stat_h", [P, 2, P], F32R)
        stat_l = s3("stat_l", [P, 2, P], F32R)
        cand = s3("cand", [P, 2, NC])
        cand_at = s3("cand_at", [P, GT, NC], U32)
        cand_f = s3("cand_f", [P, GT, NC])
        pick = s3("pick", [P, GT, NC])
        topv = s3("topv", [P, GT, TOP])
        top_at = s3("top_at", [P, GT, TOP], U32)
        top_f = s3("top_f", [P, GT, KNN])
        nb_f = s3("nb_f", [P, GT, KNN])
        v_g = s3("v_g", [P, GT, KNN])
        r_g = s3("r_g", [P, GT, KNN])
        s_g = s3("s_g", [P, GT, KNN])
        sum_a = s3("sum_a", [P, GT])
        sum_b = s3("sum_b", [P, GT])
        d2_g = s3("d2_g", [P, GT])

        right.close()
        right = ExitStack()
        sr = maker(right)
        gsum = sr("gsum", [P, NT * D], F32, "right")
        rows4 = sr("rows4", [P, 2, 4 * KNN, D], F32, "right")
        idx_c = sr("idx_c", [P, 2, 4 * KNN], U32, "right")
        s_c = sr("s_c", [P, 2, 4 * KNN], F32, "right")
        ofin = sr("ofin", [P, 2, IBS, BLK], F32, "right")
        xb = sr("xb", [P, 2, GT, D], F32, "right")
        res = sr("res", [P, GT, D], F32, "right")
        y_out = sr("y_out", [P, 2, GT, D], F32, "right")
        d2_f = sr("d2_f", [P, GT], F32, "right")
        stats = sr("stats", [P, GT, 6], F32, "right")
        mv = sr("mv", [P, GT, 2], F32, "right")
        sd = sr("sd", [P, GT], F32, "right")
        rstd = sr("rstd", [P, GT], F32, "right")
        eps_c = sr("eps_c", [P, 1], F32, "right")
        right.close()
        scope.close()

        block = whole.enter_context(nc.Block())

        def apart(eng):
            eng.sem_inc(wait_carrier, 1)

        pass2 = [(ib, jb) for ib in range(NB) for jb in range(ib, NB)]
        LAND1 = 16 * NB

        @block.sync
        def _(sp):
            for dst, src in ((w1, W1), (w2, W2)):
                sp.dma_start(dst[:], src).then_inc(consts_loaded, 16)
            for dst, src in ((b1b, b1), (b2b, b2)):
                sp.dma_start(dst[:], src.partition_broadcast(P)).then_inc(consts_loaded, 16)

            for jb in range(NB):
                sp.dma_start(ring1[:, jb, :], adjb[0, jb]).then_inc(loaded[jb], 16)
                if jb == 0:
                    sp.dma_start(y1[:].rearrange("p (t f) -> p t f", f=D), x_t).then_inc(consts_loaded, 16)
            with sp.Fori(1, NB) as ib:
                for jb in range(NB):
                    if jb == 0:
                        sp.wait_ge(p1_rows, ib)
                    if jb != 1:
                        sp.wait_ge(rows_added, (NB - 1) * (ib - 1) + max(jb, 1))
                    sp.dma_start(ring1[:, jb, :], adjb[ib, jb]).then_inc(loaded[jb], 16)

            for m, (ib, jb) in enumerate(pass2):
                if m < R2:
                    sp.wait_ge(rows_added, (NB - 1) * (NB - 1) + max(m, 1))
                    sp.wait_ge(p1_tail, m + 1)
                else:
                    was_ib, was_jb = pass2[m - R2]
                    if was_jb == NB - 1:
                        sp.wait_ge(p2_rows, was_ib + 1)
                    else:
                        sp.wait_ge(p2_blocks, m - R2 + 1 - was_ib)
                sp.dma_start(ring2[:, m % R2, :], adjb[ib, jb]).then_inc(loaded[m % R2], 16)

            sp.wait_ge(p2_rows, NB)
            sp.wait_ge(zl_done, NB)
            with sp.Fori(0, NG) as g:
                with sp.Fori(0, GT) as q:
                    for c in range(IBS):
                        sp.wait_ge(prod_ready, (g * GT + q) * IBS + c + 1)
                        sp.dma_start(a_ring[:, c, :].rearrange("p (b w) -> p b w", w=WB),
                                     adjb[q * IBS + c, ds(g * BPG, BPG)].rearrange("b p w -> p b w")
                                     ).then_inc(a_loaded[c], 16)

        @block.gpsimd
        def _(pool):
            n = [0]

            def made(ins):
                n[0] += 1
                ins.then_inc(pool_consts, 1)

            made(pool.memset(ident[:], 0.0))
            made(pool.memset(identb[:], 0.0))
            made(pool.memset(onesb[:], 1.0))
            made(pool.memset(ones[:], 1.0))
            made(pool.memset(half[:], 0.5))
            made(pool.memset(neghalf[:], -0.5))
            made(pool.iota(iota_i[:, 0:NC], pattern=[[1, NC]], base=0, channel_multiplier=0))
            made(pool.iota(iota_i[:, NC:2 * NC], pattern=[[QW, NQ], [0, TOP]], base=0, channel_multiplier=0))
            pool.wait_ge(pool_consts, n[0])
            made(pool.tensor_copy(iota_c[:], iota_i[:, 0:NC]))
            made(pool.tensor_copy(quarter_at[:], iota_i[:, NC:2 * NC]))
            for m in (ident, identb):
                made(pool.affine_select(out=m[:], in_=m[:], compare_op=ALU.not_equal, fill=1.0, base=0,
                                        pattern=[[-1, P]], channel_multiplier=1))
            pool.memset(aggT[:, 0:BLK], 0.0).then_inc(agg_zeroed, 1)

            with pool.Fori(0, NB) as ib:
                pool.wait_ge(rs_ready, ib + 1)
                pool.tensor_tensor(d1_c[:], rs_c[:], neghalf[:, 0:TPB], ALU.pow).then_inc(d1_ready, 1)

            pool.wait_ge(rowsum_ready, NB)
            pool.wait_ge(p1_rows, NB)
            pool.memset(sqrow[:], 0.0).then_inc(sqrow_zeroed, 1)
            pool.wait_ge(usum_ready, NB)
            pool.memset(aggT[:], 0.0).then_inc(agg_zeroed, 1)

            with pool.Fori(0, NG) as g:
                pool.wait_ge(v_ready, g + 1)
                pool.tensor_tensor(r_g[:].rearrange("p a b -> p (a b)"), v_g[:].rearrange("p a b -> p (a b)"),
                                   half[:], ALU.pow).then_inc(r_ready, 1)
                pool.wait_ge(s_ready, g + 1)
                pool.tensor_copy(s_all[:, ds(g * (GT * KNN), GT * KNN)], s_g[:].rearrange("p a b -> p (a b)"))
                pool.tensor_tensor(sum_a[:], s_g[:, :, 0], s_g[:, :, 1], ALU.add).then_inc(pool_step, 1)
                pool.tensor_tensor(sum_b[:], s_g[:, :, 2], s_g[:, :, 3], ALU.add).then_inc(pool_step, 1)
                pool.wait_ge(pool_step, 5 * g + 2)
                pool.tensor_tensor(sum_a[:], sum_a[:], sum_b[:], ALU.add).then_inc(pool_step, 1)
                pool.wait_ge(pool_step, 5 * g + 3)
                pool.tensor_tensor(sum_b[:], sum_a[:], rs_all[:, ds(g * GT, GT)], ALU.add).then_inc(pool_step, 1)
                pool.wait_ge(pool_step, 5 * g + 4)
                pool.wait_ge(yw_done, g + 1)
                pool.tensor_tensor(d2_g[:], sum_b[:], neghalf[:], ALU.pow).then_inc(pool_step, 1)
                pool.wait_ge(pool_step, 5 * g + 5)
                pool.tensor_copy(d2_all[:, ds(g * GT, GT)], d2_g[:])
                pool.wait_ge(xg_loaded, 16 * (g + 1))
                pool.wait_ge(ycur_ready, g + 1)
                pool.tensor_tensor(ystage[:], x_g[:], d2_g[:].unsqueeze(2).to_broadcast([P, GT, D]),
                                   ALU.mult).then_inc(ystage_ready, 1)
                pool.wait_ge(yw_done, g + 2)
                pool.dma_start(yw_t[:, ds(g * GT, GT), :], xw_g[:].rearrange("p (t f) -> p t f", f=D)
                               ).then_inc(yw_stored, 16)

            pool.wait_ge(gram_ready, NH * NT)
            pool.memset(eps_c[:], EPS_LN).then_inc(pool_consts, 1)
            pool.wait_ge(nb_ready, NG)
            pool.wait_ge(yw_stored, 16 * NG)
            with pool.Fori(0, (NT // 4) // 2) as half_s:
                s = half_s * 2
                for par in range(2):
                    pool.wait_ge(gsum_done, s + par + 1)
                    pool.tensor_copy(idx_c[:, par, :], nb_all[:, ds((s + par) * (4 * KNN), 4 * KNN)]
                                     ).then_inc(idx_ready, 1)
                    pool.wait_ge(idx_ready, s + par + 1)
                    apart(pool)
                    for k in range(4 * KNN):
                        pool.indirect_dma_start(
                            rows4[:, par, k, :], None, yw_table,
                            bass.IndirectOffsetOnAxis(ap=idx_c[:, par, k:k + 1], axis=0)
                        ).then_inc(gathered[par], 16)

        @block.scalar
        def _(act):
            for count in (gram_free, quarter_ready, ycur_ready):
                act.sem_inc(count, 1)
            for count in y_stored:
                act.sem_inc(count, 16)
            act.wait_ge(consts_loaded, 5 * 16)

            def row1(ib, first):
                if not first:
                    act.wait_ge(p1_rows, ib + 1)
                    act.activation(aggT[:, ds(ib * BLK, BLK)], pp[:, 0, :], ACT.Copy).then_inc(agg_saved, 1)
                act.wait_ge(rowsum_ready, ib + 1)
                act.activation(rs_c[:], ps_rs[:, 0:TPB], ACT.Copy).then_inc(rs_ready, 1)
                act.activation(rs_all[:, ds(ib * TPB, TPB)], ps_rs[:, 0:TPB], ACT.Copy)
                act.wait_ge(d1_ready, ib + 1)
                for k in range(TPB):
                    ys = y1[:, ds(ib * WB // TPB + k * D, D)]
                    act.activation(ys, ys, ACT.Copy, scale=d1_c[:, k:k + 1])
                act.activation(d1_all[:, ds(ib * TPB, TPB)], d1_c[:], ACT.Copy).then_inc(y1_ready, 1)

            row1(0, True)
            with act.Fori(1, NB) as ib:
                row1(ib, False)

            act.wait_ge(sqrow_zeroed, 1)
            with act.Fori(0, NB) as ib:
                act.wait_ge(zt_ready, ib + 2)
                act.activation(zTh[:, ds(ib * BLK, BLK)], ps_zt, ACT.Copy).then_inc(zh_done, 1)
                act.activation(sqrow[0:3, ds(ib * BLK, BLK)], ps_sq[0:3, :], ACT.Copy).then_inc(sqrow_done, 1)

            def stationary(t, par):
                for dst, src in ((stat_h, zTh), (stat_l, zTl)):
                    ins = act.activation(dst[:, par, :], src[:, ds(t * P, P)].bitcast(F32), ACT.Copy)
                ins.then_inc(stat_ready, 1)

            def scores(t, par, last=False):
                for h in range(NH):
                    act.wait_ge(gram_ready, t * NH + h + 1)
                    q = h // 2
                    if h % 2 == 0:
                        act.wait_ge(quarter_free, t * NQ + q + 1)
                    ins = act.activation(keys[:, q, (h % 2) * HW:(h % 2 + 1) * HW],
                                         gb[:, 2 * (h % 2):2 * (h % 2) + 2, :].rearrange("p a b -> p (a b)"),
                                         ACT.Copy)
                    ins.then_inc(gram_free, 1) if h % 2 == 0 else ins.then_inc(quarter_ready, 1)
                    if h == 0 and not last:
                        stationary(t + 1, 1 - par)

            def load_group(g):
                if not isinstance(g, int) or g > 0:
                    act.wait_ge(ystage_ready, g)
                    act.wait_ge(yw_stored, 16 * g)
                act.dma_start(x_g[:], x_t[:, ds(g * GT, GT), :]).then_inc(xg_loaded, 16)
                act.dma_start(xw_g[:], xT[:, ds(g * (GT * P), GT * P)]).then_inc(xtg_loaded, 16)

            def exp_group(g):
                act.wait_ge(r_ready, g + 1)
                if not isinstance(g, int) or g > 0:
                    act.wait_ge(ystage_ready, g)
                act.activation(s_g[:].rearrange("p a b -> p (a b)"), r_g[:].rearrange("p a b -> p (a b)"),
                               ACT.Exp, scale=-0.5).then_inc(s_ready, 1)

            def next_rows(g):
                act.wait_ge(ystage_ready, g + 1)
                act.wait_ge(prod_ready, (g * GT + 1) * IBS)
                act.activation(ycur[:], ystage[:].rearrange("p t f -> p (t f)"), ACT.Copy).then_inc(ycur_ready, 1)

            def group(g, product, first=False, last=False):
                if product:
                    next_rows(g - LAG)
                scores(g * GT, 0)
                scores(g * GT + 1, 1)
                if not first:
                    exp_group(g - 1)
                    load_group(g - 1)
                pairs = GT - 2 if not last else GT - 4
                with act.Fori(0, pairs // 2) as half_k:
                    k = half_k * 2
                    scores(g * GT + 2 + k, 0)
                    scores(g * GT + 3 + k, 1)
                if last:
                    scores(g * GT + GT - 2, 0)
                    scores(g * GT + GT - 1, 1, last=True)

            act.wait_ge(zl_done, NB)
            stationary(0, 0)
            group(0, False, first=True)
            group(1, False)
            with act.Fori(LAG, NG - 1) as g:
                group(g, True)
            group(NG - 1, True, last=True)
            next_rows(NG - 2)
            exp_group(NG - 1)
            load_group(NG - 1)
            next_rows(NG - 1)

            def norm_load(q, par):
                act.dma_start(xb[:, par], x_t[:, ds(q * GT, GT), :]).then_inc(xb_loaded[par], 16)

            act.wait_ge(gram_ready, NH * NT)
            act.wait_ge(pool_consts, 13)
            def finish(q, par, more):
                act.wait_ge(var_ready, q + 1)
                act.activation(sd[:], mv[:, :, 1], ACT.Sqrt, bias=eps_c[:]).then_inc(sd_ready, 1)
                act.wait_ge(y_ready, q + 1)
                act.dma_start(out_t[:, ds(q * GT, GT), :], y_out[:, par]).then_inc(y_stored[par], 16)
                if more:
                    norm_load(q + 2, par)

            norm_load(0, 0)
            norm_load(1, 1)
            with act.Fori(0, (GT - 2) // 2) as half_q:
                q = half_q * 2
                finish(q, 0, True)
                finish(q + 1, 1, True)
            finish(GT - 2, 0, False)
            finish(GT - 1, 1, False)
            for par in range(2):
                act.wait_ge(y_stored[par], 16 * (GT // 2 + 1))

        @block.tensor
        def _(pe):
            pe.wait_ge(pool_consts, 12)

            for count in (p1_rows, z_ready, zt_ready):
                pe.sem_inc(count, 1)

            for ib in range(NB):
                if ib >= 2:
                    pe.wait_ge(agg_saved, ib - 1)
                for jb in range(ib):
                    pe.wait_ge(loaded[jb], 16 * (ib + 1))
                    if jb == ib - 1:
                        pe.wait_ge(y1_ready, ib)
                    for jt in range(TPB):
                        mm = pe.matmul(pp[:, 0, :], y1[:, (jb * TPB + jt) * D:(jb * TPB + jt + 1) * D],
                                       ring1[:, jb, jt * BLK:(jt + 1) * BLK],
                                       start=(jb == 0 and jt == 0), stop=(jb == ib - 1 and jt == TPB - 1))
                    if jb == ib - 1:
                        mm.then_inc(p1_rows, 1)
                    elif ib == NB - 1 and jb < R2:
                        mm.then_inc(p1_tail, 1)
                pe.wait_ge(rows_added, (NB - 1) * (ib + 1))
                if ib >= 1:
                    pe.wait_ge(y1_ready, ib)
                for it in range(TPB):
                    for jt in range(TPB):
                        mm = pe.matmul(ps_rs[:, it:it + 1], acc[:, jt * BLK + it * P:jt * BLK + (it + 1) * P],
                                       ones[:], start=(jt == 0), stop=(jt == TPB - 1))
                mm.then_inc(rowsum_ready, 1)

            def z_product(r):
                pe.wait_ge(usum_ready, r + 1)
                if r >= 1:
                    pe.wait_ge(z_done, r)
                for it in range(TPB):
                    mm = pe.matmul(ps_z[:, it * D:(it + 1) * D], usum[:, it * P:(it + 1) * P], w1[:],
                                   start=True, stop=True)
                mm.then_inc(z_ready, 1)

            def z_transpose(r):
                pe.wait_ge(z_done, r + 1)
                if r >= 1:
                    pe.wait_ge(zl_done, r)
                    pe.wait_ge(sqrow_done, r)
                for it in range(TPB):
                    pe.transpose(ps_zt[:, it * P:(it + 1) * P], z_c[:, it, :], ident[:])
                for it in range(TPB):
                    mm = pe.matmul(ps_sq[0:3, it * P:(it + 1) * P], sq_parts[:, it, :], identb[:],
                                   start=True, stop=True)
                mm.then_inc(zt_ready, 1)

            pe.wait_ge(agg_saved, NB - 1)
            pe.wait_ge(y1_ready, NB)
            for m, (ib, jb) in enumerate(pass2):
                if jb == ib and ib >= 2:
                    pe.wait_ge(usum_ready, ib - 1)
                pe.wait_ge(loaded[m % R2], LAND1 + 16 * (m // R2 + 1))
                for jt in range(TPB):
                    mm = pe.matmul(pp[:, ib % 2, :], y1[:, (jb * TPB + jt) * D:(jb * TPB + jt + 1) * D],
                                   ring2[:, m % R2, jt * BLK:(jt + 1) * BLK],
                                   start=(jb == ib and jt == 0), stop=(jb == NB - 1 and jt == TPB - 1))
                mm.then_inc(p2_rows if jb == NB - 1 else p2_blocks, 1)
                if ib >= 1 and jb == ib:
                    z_product(ib - 1)
                if ib >= 1 and jb == min(ib + 1, NB - 1):
                    z_transpose(ib - 1)
            z_product(NB - 1)
            z_transpose(NB - 1)

            pe.wait_ge(zl_done, NB)
            pe.wait_ge(sqrow_done, NB)
            pe.sem_inc(prod_ready, IBS)

            def scores(t, par):
                pe.wait_ge(stat_ready, t + 1)
                for h in range(NH):
                    if h % 2 == 0:
                        pe.wait_ge(gram_free, t * NQ + h // 2 + 1)
                    else:
                        pe.wait_ge(quarter_ready, t * NQ + h // 2 + 1)
                    for c in range(2):
                        bank = gb[:, 2 * (h % 2) + c, :]
                        cols = slice((2 * h + c) * BLK, (2 * h + c + 1) * BLK)
                        pe.matmul(bank, stat_h[:, par, :], zTh[:, cols], start=True, stop=False)
                        pe.matmul(bank, stat_h[:, par, :], zTl[:, cols], start=False, stop=False)
                        pe.matmul(bank, stat_l[:, par, :], zTh[:, cols], start=False, stop=False)
                        mm = pe.matmul(bank, onesb[:], sqrow[:, cols], start=False, stop=True)
                    mm.then_inc(gram_ready, 1)

            def product(s, c, last=False):
                pe.wait_ge(a_loaded[c], (s + 1) * 16)
                if last:
                    pe.wait_ge(ofin_ready, (s - (NG - 1) * GT - 1) * IBS + c + 1)
                else:
                    pe.wait_ge(prod_free, s * IBS + c + 1)
                for jt in range(GT):
                    mm = pe.matmul(pp[:, c, :], ycur[:, jt * D:(jt + 1) * D],
                                   a_ring[:, c, jt * BLK:(jt + 1) * BLK], start=(jt == 0), stop=(jt == GT - 1))
                mm.then_inc(prod_ready, 1)

            def x_w2(g):
                pe.wait_ge(xtg_loaded, 16 * (g + 1))
                pe.wait_ge(yw_done, g + 1)
                for k in range(GT):
                    mm = pe.matmul(px[:, k // TPB, (k % TPB) * D:(k % TPB + 1) * D], xw_g[:, k * P:(k + 1) * P],
                                   w2[:], start=True, stop=True)
                mm.then_inc(psx_ready, 1)

            with pe.Fori(0, GT // 2) as half_k:
                k = half_k * 2
                scores(k, 0)
                scores(k + 1, 1)
            with pe.Fori(0, GT // 2) as half_k:
                k = half_k * 2
                scores(k + GT, 0)
                scores(k + GT + 1, 1)
            x_w2(0)
            with pe.Fori(LAG, NG) as g:
                with pe.Fori(0, GT // 2) as half_k:
                    k = half_k * 2
                    for par in range(2):
                        scores(g * GT + k + par, par)
                        pe.wait_ge(ycur_ready, g - LAG + 2)
                        for c in range(IBS):
                            product((g - LAG) * GT + k + par, c)
                x_w2(g - 1)
            pe.wait_ge(ycur_ready, NG - LAG + 2)
            for c in range(IBS):
                product((NG - LAG) * GT, c)
            x_w2(NG - 1)
            with pe.Fori(1, GT) as k:
                for c in range(IBS):
                    product((NG - LAG) * GT + k, c)

            def last_product(q, par):
                pe.wait_ge(ofin_ready, IBS * (q + 1))
                pe.wait_ge(fin_step, q + 1)
                for c in range(IBS):
                    for it in range(TPB):
                        mm = pe.matmul(px[:, c, it * D:(it + 1) * D], ofin[:, par, c, it * P:(it + 1) * P],
                                       w2[:], start=True, stop=True)
                mm.then_inc(fin_ready, 1)

            end = (NG - 1) * GT
            pe.wait_ge(ycur_ready, NG + 1)
            product(end, 0)
            product(end, 1)
            product(end + 1, 0, last=True)
            last_product(0, 0)
            product(end + 1, 1, last=True)
            with pe.Fori(1, GT // 2) as half_q:
                q = half_q * 2
                for par in range(2):
                    product(q + end + par, 0, last=True)
                    last_product(q + par - 1, 1 - par)
                    product(q + end + par, 1, last=True)
            last_product(GT - 1, 1)

        @block.vector
        def _(dve):
            dve.sem_inc(yw_done, 1)

            def add_row(ib, first):
                for jb in range(1, NB):
                    if jb == 1:
                        dve.wait_ge(loaded[0], (ib + 1) * 16)
                        if not first:
                            dve.wait_ge(rowsum_ready, ib)
                    else:
                        dve.wait_ge(rows_added, ib * (NB - 1) + jb - 1)
                    dve.wait_ge(loaded[jb], (ib + 1) * 16)
                    dve.tensor_tensor(acc[:], ring1[:, 0, :] if jb == 1 else acc[:], ring1[:, jb, :],
                                      ALU.add).then_inc(rows_added, 1)

            add_row(0, True)
            with dve.Fori(1, NB) as ib:
                add_row(ib, False)

            dve.wait_ge(agg_zeroed, 1)
            dve.wait_ge(p1_rows, NB)
            dve.wait_ge(consts_loaded, 5 * 16)
            with dve.Fori(0, NB // 2) as half_two:
                two = half_two * 2
                for par in range(2):
                    ib = two + par
                    at = 11 * ib
                    dve.wait_ge(p2_rows, ib + 1)
                    dve.wait_ge(z_ready, ib + 1)
                    dve.tensor_tensor(usum[:], pp[:, par, :], aggT[:, ds(ib * BLK, BLK)],
                                      ALU.add).then_inc(usum_ready, 1)
                    dve.tensor_copy(d1_z[:], d1_all[:, ds(ib * TPB, TPB)]).then_inc(zstep, 1)
                    dve.wait_ge(zstep, at + 1)
                    dve.wait_ge(z_ready, ib + 2)
                    dve.wait_ge(zt_ready, ib + 1)
                    for it in range(TPB):
                        dve.scalar_tensor_tensor(out=z_c[:, it, :], in0=ps_z[:, it * D:(it + 1) * D],
                                                 scalar=d1_z[:, it:it + 1], in1=b1b[:], op0=ALU.mult,
                                                 op1=ALU.add).then_inc(zstep, 1)
                    zf = z_c[:].rearrange("p a b -> p (a b)")
                    dve.wait_ge(zstep, at + 5)
                    dve.scalar_tensor_tensor(out=zf, in0=zf, scalar=0.1, in1=zf, op0=ALU.mult,
                                             op1=ALU.max).then_inc(zstep, 1)
                    dve.wait_ge(zstep, at + 6)
                    for it in range(TPB):
                        ins = dve.tensor_tensor_reduce(out=junk[:, it, :], in0=z_c[:, it, :], in1=z_c[:, it, :],
                                                       scale=1.0, scalar=0.0, op0=ALU.mult, op1=ALU.add,
                                                       accum_out=sq_c[:, it:it + 1])
                    ins.then_inc(zstep, 1)
                    dve.wait_ge(zstep, at + 7)
                    dve.tensor_copy(sq_all[:, ds(ib * TPB, TPB)], sq_c[:])
                    dve.tensor_scalar(sq_parts[:, :, 0], sq_c[:], -0.5, None, ALU.mult).then_inc(zstep, 1)
                    dve.wait_ge(zstep, at + 8)
                    dve.scalar_tensor_tensor(out=sq_r[:], in0=sq_c[:], scalar=-0.5, in1=sq_parts[:, :, 0],
                                             op0=ALU.mult, op1=ALU.subtract).then_inc(zstep, 1)
                    dve.wait_ge(zstep, at + 9)
                    dve.tensor_copy(sq_parts[:, :, 1], sq_r[:]).then_inc(zstep, 1)
                    dve.wait_ge(zstep, at + 10)
                    dve.tensor_tensor(sq_r[:], sq_r[:], sq_parts[:, :, 1], ALU.subtract).then_inc(zstep, 1)
                    dve.wait_ge(zstep, at + 11)
                    dve.tensor_copy(sq_parts[:, :, 2], sq_r[:]).then_inc(z_done, 1)
                    dve.wait_ge(zh_done, ib + 1)
                    cols = ds(ib * BLK, BLK)
                    dve.tensor_tensor(zTl[:, cols], ps_zt, zTh[:, cols].bitcast(F32),
                                      ALU.subtract).then_inc(zl_done, 1)

            dve.sem_inc(quarter_free, NQ)
            dve.sem_inc(prod_free, IBS)

            def neighbours(g, k):
                at = (g * GT + k) * (NQ + 1)
                for q in range(NQ):
                    dve.wait_ge(quarter_ready, (g * GT + k) * NQ + q + 2)
                    c8 = cand[:, k % 2, q * TOP:(q + 1) * TOP]
                    apart(dve)
                    dve.max(c8, keys[:, q, :]).then_inc(knn_step, 1)
                    dve.wait_ge(knn_step, at + q + 1)
                    apart(dve)
                    dve.max_index(cand_at[:, k, q * TOP:(q + 1) * TOP], c8, keys[:, q, :]
                                  ).then_inc(quarter_free, 1)
                dve.max(topv[:, k, :], cand[:, k % 2, :]).then_inc(knn_step, 1)
                dve.wait_ge(knn_step, at + NQ + 1)
                apart(dve)
                dve.max_index(top_at[:, k, :], topv[:, k, :], cand[:, k % 2, :])

            def add_product(s, q, c):
                dve.wait_ge(prod_ready, s * IBS + c + 1 + IBS)
                cols = q * IBS * BLK + c * BLK
                cols = ds(cols, BLK) if not isinstance(cols, int) else slice(cols, cols + BLK)
                dve.tensor_tensor(aggT[:, cols], aggT[:, cols], pp[:, c, :], ALU.add).then_inc(prod_free, 1)

            def distances(g):
                at = g * 16
                if not isinstance(g, int) or g > 0:
                    dve.wait_ge(r_ready, g)
                dve.wait_ge(knn_step, (g * GT + GT) * (NQ + 1))
                sq = sq_all[:, ds(g * GT, GT)].unsqueeze(2).to_broadcast([P, GT, KNN])
                dve.scalar_tensor_tensor(out=v_g[:], in0=topv[:, :, 0:KNN], scalar=-2.0, in1=sq,
                                         op0=ALU.mult, op1=ALU.add).then_inc(grp_step, 1)
                dve.wait_ge(grp_step, at + 1)
                dve.tensor_scalar(v_g[:], v_g[:], 0.0, EPS_D2, ALU.max, ALU.add).then_inc(v_ready, 1)
                dve.tensor_copy(top_f[:], top_at[:, :, 0:KNN]).then_inc(grp_step, 1)
                dve.tensor_copy(cand_f[:], cand_at[:]).then_inc(grp_step, 1)
                dve.wait_ge(grp_step, at + 3)
                dve.tensor_tensor(cand_f[:], cand_f[:], quarter_at[:].unsqueeze(1).to_broadcast([P, GT, NC]),
                                  ALU.add).then_inc(grp_step, 1)
                dve.wait_ge(grp_step, at + 4)
                for k in range(KNN):
                    if k:
                        dve.wait_ge(grp_step, at + 4 + 3 * k)
                    dve.tensor_tensor(pick[:], iota_c[:].unsqueeze(1).to_broadcast([P, GT, NC]),
                                      top_f[:, :, k:k + 1].to_broadcast([P, GT, NC]), ALU.is_equal
                                      ).then_inc(grp_step, 1)
                    dve.wait_ge(grp_step, at + 5 + 3 * k)
                    dve.tensor_tensor(pick[:], pick[:], cand_f[:], ALU.mult).then_inc(grp_step, 1)
                    dve.wait_ge(grp_step, at + 6 + 3 * k)
                    dve.tensor_reduce(nb_f[:, :, k], pick[:], AX_X, ALU.add).then_inc(grp_step, 1)
                dve.wait_ge(grp_step, at + 16)
                dve.tensor_copy(nb_all[:, ds(g * (GT * KNN), GT * KNN)], nb_f[:].rearrange("p a b -> p (a b)")
                                ).then_inc(nb_ready, 1)

            def table_rows(g):
                dve.wait_ge(psx_ready, g + 1)
                dve.wait_ge(ystage_ready, g + 1)
                for c in range(2):
                    ins = dve.tensor_tensor(
                        xw_g[:, c * BLK:(c + 1) * BLK].rearrange("p (t f) -> p t f", f=D),
                        px[:, c, :].rearrange("p (t f) -> p t f", f=D),
                        d2_g[:, c * TPB:(c + 1) * TPB].unsqueeze(2).to_broadcast([P, TPB, D]), ALU.mult)
                ins.then_inc(yw_done, 1)

            def group(g, product):
                for k in range(GT):
                    neighbours(g, k)
                    if product:
                        for c in range(IBS):
                            add_product((g - LAG) * GT + k, k, c)
                distances(g)

            dve.wait_ge(pool_consts, 12)
            group(0, False)
            group(1, False)
            table_rows(0)
            dve.wait_ge(agg_zeroed, 2)
            with dve.Fori(LAG, NG) as g:
                group(g, True)
                table_rows(g - 1)

            dve.wait_ge(gram_ready, NH * NT)
            dve.sem_inc(gsum_done, 2)

            def sum_neighbours(s, par):
                dve.tensor_copy(s_c[:, par, :], s_all[:, ds(s * (4 * KNN), 4 * KNN)]).then_inc(scal_ready, 1)
                dve.wait_ge(scal_ready, s + 1)
                dve.wait_ge(gathered[par], (s - par) * (4 * KNN * 8) + 16 * 4 * KNN)
                for k in range(KNN):
                    if k:
                        dve.wait_ge(gs_step, s * 3 + k)
                    for i in range(4):
                        to = gsum[:, ds(s * (4 * D) + i * D, D)]
                        j = i * KNN + k
                        if k == 0:
                            ins = dve.tensor_scalar(to, rows4[:, par, j, :], s_c[:, par, j:j + 1], None, ALU.mult)
                        else:
                            ins = dve.scalar_tensor_tensor(out=to, in0=rows4[:, par, j, :],
                                                           scalar=s_c[:, par, j:j + 1], in1=to,
                                                           op0=ALU.mult, op1=ALU.add)
                    ins.then_inc(gsum_done if k == KNN - 1 else gs_step, 1)

            s0 = (NG - LAG) * GT
            add_product(s0, 0, 0)
            add_product(s0, 0, 1)
            table_rows(NG - 1)
            dve.wait_ge(yw_done, NG + 1)
            dve.sem_inc(fin_step, 1)
            sum_neighbours(0, 0)
            add_product(s0 + 1, 1, 0)
            add_product(s0 + 1, 1, 1)
            sum_neighbours(1, 1)
            with dve.Fori(1, GT // 2) as half_q:
                q = half_q * 2
                for par in range(2):
                    add_product(q + s0 + par, q + par, 0)
                    add_product(q + s0 + par, q + par, 1)
                    sum_neighbours(q + par, par)

            def complete(q, par):
                for c in range(IBS):
                    dve.wait_ge(prod_ready, (q + (NG - 1) * GT) * IBS + c + 1 + IBS)
                    dve.tensor_tensor(ofin[:, par, c, :], aggT[:, ds(q * (IBS * BLK) + c * BLK, BLK)],
                                      pp[:, c, :], ALU.add).then_inc(ofin_ready, 1)

            def norm(q, par):
                at = q * 5
                dve.wait_ge(fin_ready, q + 1)
                dve.wait_ge(gsum_done, 2 * q + 4)
                if not isinstance(q, int) or q > 0:
                    dve.wait_ge(y_ready, q)
                for c in range(IBS):
                    ins = dve.tensor_tensor(res[:, c * TPB:(c + 1) * TPB, :].rearrange("p t f -> p (t f)"),
                                            px[:, c, :], gsum[:, ds(q * (GT * D) + c * BLK, BLK)], ALU.add)
                ins.then_inc(fin_step, 1)
                dve.tensor_copy(d2_f[:], d2_all[:, ds(q * GT, GT)]).then_inc(norm_step, 1)
                dve.wait_ge(xb_loaded[par], (q - par) * 8 + 16)
                dve.tensor_tensor(xb[:, par], xb[:, par], b2b[:].unsqueeze(1).to_broadcast([P, GT, D]),
                                  ALU.add).then_inc(norm_step, 1)
                dve.wait_ge(fin_step, q + 2)
                dve.wait_ge(norm_step, at + 2)
                for i in range(GT):
                    ins = dve.scalar_tensor_tensor(out=res[:, i, :], in0=res[:, i, :], scalar=d2_f[:, i:i + 1],
                                                   in1=xb[:, par, i, :], op0=ALU.mult, op1=ALU.add)
                ins.then_inc(norm_step, 1)
                dve.wait_ge(norm_step, at + 3)
                for i in range(GT):
                    ins = dve.bn_stats(stats[:, i, :], res[:, i, :])
                ins.then_inc(norm_step, 1)
                dve.wait_ge(norm_step, at + 4)
                apart(dve)
                for i in range(GT):
                    ins = dve.bn_aggr(mv[:, i, :], stats[:, i, :])
                ins.then_inc(var_ready, 1)
                dve.wait_ge(sd_ready, q + 1)
                dve.reciprocal(rstd[:], sd[:]).then_inc(norm_step, 1)
                dve.wait_ge(norm_step, at + 5)
                dve.wait_ge(y_stored[par], (q - par) * 8 + 16)
                for i in range(GT):
                    ins = dve.tensor_scalar(y_out[:, par, i, :], res[:, i, :], mv[:, i, 0:1], rstd[:, i:i + 1],
                                            ALU.subtract, ALU.mult)
                ins.then_inc(y_ready, 1)

            complete(0, 0)
            sum_neighbours(GT, 0)
            complete(1, 1)
            sum_neighbours(GT + 1, 1)
            norm(0, 0)
            with dve.Fori(1, GT // 2) as half_q:
                q = half_q * 2
                for par in range(2):
                    complete(q + par, par)
                    sum_neighbours(q + (GT + par), par)
                    norm(q + (par - 1), 1 - par)
            norm(GT - 1, 1)


def kernel(x, adj, L0_gnn_W1, L0_gnn_b1, L0_gnn_W2, L0_gnn_b2):
    import numpy as np
    import concourse.bacc as bacc
    from concourse.bass_utils import run_bass_kernel_spmd

    x, adj = np.asarray(x), np.asarray(adj)
    nb = adj.shape[0] // BLK
    arrays = {
        "x": np.ascontiguousarray(x),
        "xT": np.ascontiguousarray(x.T),
        "adjb": np.ascontiguousarray(
            adj.reshape(nb, BLK, nb, TPB, P).transpose(0, 2, 4, 3, 1)).reshape(nb, nb, P, TPB * BLK),
        "W1": np.ascontiguousarray(L0_gnn_W1), "b1": np.ascontiguousarray(L0_gnn_b1),
        "W2": np.ascontiguousarray(L0_gnn_W2), "b2": np.ascontiguousarray(L0_gnn_b2),
    }
    nc = bacc.Bacc("TRN2", target_bir_lowering=False, num_devices=1)
    args = {n: nc.dram_tensor(n, a.shape, mybir.dt.from_np(a.dtype), kind="ExternalInput").ap()
            for n, a in arrays.items()}
    args["out"] = nc.dram_tensor("out", x.shape, F32, kind="ExternalOutput").ap()
    gnn_resnorm(nc, **args)
    r = run_bass_kernel_spmd(nc, [arrays], core_ids=[0])
    return r.results[0]["out"]
```

```python
from contextlib import ExitStack

import concourse.bass as bass
from concourse import mybir

F32 = mybir.dt.float32
F32R = mybir.dt.float32r
BF16 = mybir.dt.bfloat16
U32 = mybir.dt.uint32
I32 = mybir.dt.int32
ALU = mybir.AluOpType
ACT = mybir.ActivationFunctionType
AX_X = mybir.AxisListType.X

P = 128
BLK = 512
TPB = BLK // P
GT = 8
KNN = 4
TOP = 8
LAG = 2
EPS_D2 = 1e-10
EPS_LN = 1e-5
ds = bass.ds


def gnn_resnorm(nc, x, xT, adjb, W1, b1, W2, b2, out):
    N, D = x.shape
    NT = N // P
    NB = N // BLK
    NG = NT // GT
    BPG = GT // TPB
    IBS = NB // GT
    QW = 2048
    NQ = N // QW
    HW = 2 * BLK
    NH = N // HW
    NC = NQ * TOP
    R2 = 6
    WB = TPB * BLK
    assert D == P and IBS == 2 and NB == 16 and NG > LAG + 1

    x_t = x.rearrange("(t p) f -> p t f", p=P)
    out_t = out.rearrange("(t p) f -> p t f", p=P)
    yw_table = nc.dram_tensor("yw_table", (N, D), F32, kind="Internal").ap()
    yw_t = yw_table.rearrange("(t p) f -> p t f", p=P)

    whole = ExitStack()
    with whole:
        def maker(stack):
            return lambda name, shape, dt=F32, side=None: stack.enter_context(
                nc.sbuf_tensor(name, shape, dt, **({"side": side} if side else {})))

        def sem(name):
            return whole.enter_context(nc.semaphore(name))

        def psum(name, shape):
            return whole.enter_context(nc.psum_tensor(name, shape, F32))

        sb = maker(whole)
        aggT = sb("aggT", [P, N])
        y1 = sb("y1", [P, NT * D])
        w1 = sb("w1", [P, D])
        w2 = sb("w2", [P, D])
        b1b = sb("b1b", [P, D])
        ident = sb("ident", [P, P])
        ones = sb("ones", [P, P])
        half = sb("half", [P, GT * KNN])
        neghalf = sb("neghalf", [P, GT])
        iota_c = sb("iota_c", [P, NC])
        quarter_at = sb("quarter_at", [P, NC])
        rs_all = sb("rs_all", [P, NT])
        d1_all = sb("d1_all", [P, NT])
        d2_all = sb("d2_all", [P, NT])
        sq_all = sb("sq_all", [P, NT])
        s_all = sb("s_all", [P, NT * KNN])
        nb_all = sb("nb_all", [P, NT * KNN], U32)
        rs_c = sb("rs_c", [P, TPB])
        d1_c = sb("d1_c", [P, TPB])

        gb = psum("gb", [P, 4, BLK])
        pp = psum("pp", [P, 2, BLK])
        px = psum("px", [P, 2, BLK])
        ps_rs, ps_z, ps_zt = (gb[:, k, :] for k in range(3))

        consts_loaded = sem("consts_loaded")
        pool_consts = sem("pool_consts")
        wait_carrier = sem("wait_carrier")
        agg_zeroed = sem("agg_zeroed")
        loaded = [sem(f"loaded{k}") for k in range(NB)]
        rows_added = sem("rows_added")
        p1_rows = sem("p1_rows")
        p1_tail = sem("p1_tail")
        rowsum_ready = sem("rowsum_ready")
        rs_ready = sem("rs_ready")
        d1_ready = sem("d1_ready")
        d1_stored = sem("d1_stored")
        y1_ready = sem("y1_ready")
        agg_saved = sem("agg_saved")
        p2_blocks = sem("p2_blocks")
        p2_rows = sem("p2_rows")
        usum_ready = sem("usum_ready")
        z_ready = sem("z_ready")
        zstep = sem("zstep")
        z_done = sem("z_done")
        zt_ready = sem("zt_ready")
        zh_done = sem("zh_done")
        zl_done = sem("zl_done")
        sq_step = sem("sq_step")
        diag_ready = sem("diag_ready")
        sqb_ready = sem("sqb_ready")
        sqb_done = sem("sqb_done")
        stat_ready = sem("stat_ready")
        gram_free = sem("gram_free")
        gram_ready = sem("gram_ready")
        quarter_ready = sem("quarter_ready")
        quarter_keyed = sem("quarter_keyed")
        quarter_free = sem("quarter_free")
        knn_step = sem("knn_step")
        grp_step = sem("grp_step")
        v_ready = sem("v_ready")
        r_ready = sem("r_ready")
        s_ready = sem("s_ready")
        pool_step = sem("pool_step")
        ystage_ready = sem("ystage_ready")
        ycur_ready = sem("ycur_ready")
        nb_ready = sem("nb_ready")
        xg_loaded = sem("xg_loaded")
        xtg_loaded = sem("xtg_loaded")
        psx_ready = sem("psx_ready")
        yw_done = sem("yw_done")
        yw_stored = sem("yw_stored")
        a_loaded = [sem(f"a_loaded{k}") for k in range(IBS * BPG)]
        block_used = sem("block_used")
        prod_ready = sem("prod_ready")
        prod_free = sem("prod_free")
        idx_ready = sem("idx_ready")
        gathered = [sem(f"gathered{k}") for k in range(2)]
        scal_ready = sem("scal_ready")
        gs_step = sem("gs_step")
        gsum_done = sem("gsum_done")
        ofin_ready = sem("ofin_ready")
        fin_ready = sem("fin_ready")
        fin_step = sem("fin_step")
        norm_step = sem("norm_step")
        xb_loaded = [sem(f"xb_loaded{k}") for k in range(2)]
        b2_loaded = sem("b2_loaded")
        var_ready = sem("var_ready")
        sd_ready = sem("sd_ready")
        y_ready = sem("y_ready")
        y_stored = [sem(f"y_stored{k}") for k in range(2)]

        scope = ExitStack()
        s1 = maker(scope)
        ring1 = s1("ring1", [P, NB, WB])
        acc = s1("acc", [P, WB])
        scope.close()

        right = ExitStack()
        sr = maker(right)
        zTh = sr("zTh", [P, N], F32R, "right")
        zTl = sr("zTl", [P, N], F32R, "right")
        scope = ExitStack()
        s2 = maker(scope)
        ring2 = s2("ring2", [P, R2, WB])
        usum = s2("usum", [P, BLK])
        z_c = s2("z_c", [P, TPB, D])
        junk = s2("junk", [P, TPB, D])
        d1_z = s2("d1_z", [P, TPB])
        sq_c = s2("sq_c", [P, TPB])
        scope.close()

        scope = ExitStack()
        s3 = maker(scope)
        keys = y1[:, :].rearrange("p (s w) -> p s w", w=QW)
        sqb = sr("sqb", [P, N], F32, "right")
        a_ring = s3("a_ring", [P, 3, WB])
        ycur = s3("ycur", [P, GT * D])
        ystage = s3("ystage", [P, GT, D])
        xw_g = s3("xw_g", [P, GT * D])
        stat_h = s3("stat_h", [P, 2, P], F32R)
        stat_l = s3("stat_l", [P, 2, P], F32R)
        cand = s3("cand", [P, 2, NC])
        cand_at = s3("cand_at", [P, GT, NC], U32)
        cand_f = cand_at[:].bitcast(F32)
        pick = s3("pick", [P, GT, NC])
        topv = s3("topv", [P, GT, TOP])
        top_at = s3("top_at", [P, GT, TOP], U32)
        top_f = s3("top_f", [P, GT, KNN])
        nb_f = s3("nb_f", [P, GT, KNN])
        v_g = s3("v_g", [P, GT, KNN])
        r_g = s3("r_g", [P, GT, KNN])
        s_g = s3("s_g", [P, GT, KNN])
        sq_c4 = s3("sq_c4", [P, 2, TPB])
        sum_a = s3("sum_a", [P, GT])
        sum_b = s3("sum_b", [P, GT])
        d2_g = s3("d2_g", [P, GT])

        right.close()
        right = ExitStack()
        sr = maker(right)
        gsum = y1
        rows4 = sr("rows4", [P, 2, 4 * KNN, D], F32, "right")
        idx_c = sr("idx_c", [P, 2, 4 * KNN], U32, "right")
        s_c = sr("s_c", [P, 2, 4 * KNN], F32, "right")
        ofin = sr("ofin", [P, 2, IBS, BLK], F32, "right")
        xb = sr("xb", [P, 2, GT, D], F32, "right")
        res = sr("res", [P, GT, D], F32, "right")
        y_out = sr("y_out", [P, 2, GT, D], F32, "right")
        d2_f = sr("d2_f", [P, GT], F32, "right")
        stats = sr("stats", [P, GT, 6], F32, "right")
        mv = sr("mv", [P, GT, 2], F32, "right")
        sd = sr("sd", [P, GT], F32, "right")
        rstd = sr("rstd", [P, GT], F32, "right")
        eps_c = sr("eps_c", [P, 1], F32, "right")
        b2b = sr("b2b", [P, D], F32, "right")
        a_tail = sr("a_tail", [P, IBS * BPG, WB], F32, "right")
        right.close()
        scope.close()

        block = whole.enter_context(nc.Block())

        def apart(eng):
            eng.sem_inc(wait_carrier, 1)

        CONSTS = 9
        pass2 = [(ib, jb) for ib in range(NB) for jb in range(ib, NB)]
        LAND1 = 16 * NB

        @block.sync
        def _(sp):
            for dst, src in ((w1, W1), (w2, W2)):
                sp.dma_start(dst[:], src).then_inc(consts_loaded, 16)
            sp.dma_start(b1b[:], b1.partition_broadcast(P)).then_inc(consts_loaded, 16)

            for jb in range(NB):
                sp.dma_start(ring1[:, jb, :], adjb[0, jb]).then_inc(loaded[jb], 16)
                if jb == 0:
                    sp.dma_start(y1[:].rearrange("p (t f) -> p t f", f=D), x_t).then_inc(consts_loaded, 16)
            with sp.Fori(1, NB) as ib:
                for jb in range(NB):
                    if jb == 0:
                        sp.wait_ge(p1_rows, ib)
                    if jb != 1:
                        sp.wait_ge(rows_added, (NB - 1) * (ib - 1) + max(jb, 1))
                    sp.dma_start(ring1[:, jb, :], adjb[ib, jb]).then_inc(loaded[jb], 16)

            for m, (ib, jb) in enumerate(pass2):
                if m < R2:
                    sp.wait_ge(rows_added, (NB - 1) * (NB - 1) + max(m, 1))
                    sp.wait_ge(p1_tail, m + 1)
                else:
                    was_ib, was_jb = pass2[m - R2]
                    if was_jb == NB - 1:
                        sp.wait_ge(p2_rows, was_ib + 1)
                    else:
                        sp.wait_ge(p2_blocks, m - R2 + 1 - was_ib)
                sp.dma_start(ring2[:, m % R2, :], adjb[ib, jb]).then_inc(loaded[m % R2], 16)

            def load_a(g, q, ring, slots):
                s = g * GT + q
                for i in range(IBS * BPG):
                    c, b = divmod(i, BPG)
                    if slots[i] == i and len(set(slots)) == 3:
                        if i == 0:
                            sp.wait_ge(prod_ready, s * IBS + IBS)
                    elif slots[i] != i:
                        sp.wait_ge(block_used, s * IBS + 1)
                    elif b == 0:
                        sp.wait_ge(block_used, s * IBS + c - 1)
                    else:
                        sp.wait_ge(prod_ready, s * IBS + c + 1)
                    sp.dma_start(ring[:, slots[i], :], adjb[q * IBS + c, g * BPG + b]).then_inc(a_loaded[i], 16)

            sp.wait_ge(p2_rows, NB)
            sp.wait_ge(zl_done, NB)
            with sp.Fori(0, NG - LAG) as g:
                with sp.Fori(0, GT) as q:
                    load_a(g, q, a_ring, (0, 1, 2, 0))
            sp.wait_ge(gram_ready, NH * NT)
            sp.wait_ge(quarter_keyed, NQ * NT)
            with sp.Fori(NG - LAG, NG) as g:
                with sp.Fori(0, GT) as q:
                    load_a(g, q, a_tail, (0, 1, 2, 3))

        @block.gpsimd
        def _(pool):
            n = [0]

            def made(ins):
                n[0] += 1
                ins.then_inc(pool_consts, 1)

            made(pool.memset(ident[:], 0.0))
            made(pool.memset(ones[:], 1.0))
            made(pool.memset(half[:], 0.5))
            made(pool.memset(neghalf[:], -0.5))
            iota_i = nb_all[:, 0:2 * NC].bitcast(I32)
            made(pool.iota(iota_i[:, 0:NC], pattern=[[1, NC]], base=0, channel_multiplier=0))
            made(pool.iota(iota_i[:, NC:2 * NC], pattern=[[QW, NQ], [0, TOP]], base=0, channel_multiplier=0))
            pool.wait_ge(pool_consts, n[0])
            made(pool.tensor_copy(iota_c[:], iota_i[:, 0:NC]))
            made(pool.tensor_copy(quarter_at[:], iota_i[:, NC:2 * NC]))
            made(pool.affine_select(out=ident[:], in_=ident[:], compare_op=ALU.not_equal, fill=1.0, base=0,
                                    pattern=[[-1, P]], channel_multiplier=1))
            assert n[0] == CONSTS
            pool.memset(aggT[:, 0:BLK], 0.0).then_inc(agg_zeroed, 1)

            with pool.Fori(0, NB) as ib:
                pool.wait_ge(rs_ready, ib + 1)
                pool.tensor_tensor(d1_c[:], rs_c[:], neghalf[:, 0:TPB], ALU.pow).then_inc(d1_ready, 1)

            pool.wait_ge(usum_ready, NB)
            pool.memset(aggT[:], 0.0).then_inc(agg_zeroed, 1)

            def add_squares(t):
                for q in range(NQ):
                    pool.wait_ge(quarter_ready, t * NQ + q + 2)
                    pool.tensor_tensor(keys[:, q, :], keys[:, q, :], sqb[:, q * QW:(q + 1) * QW], ALU.add
                                       ).then_inc(quarter_keyed, 1)

            def store_table(g):
                pool.wait_ge(yw_done, g + 2)
                pool.dma_start(yw_t[:, ds(g * GT, GT), :], xw_g[:].rearrange("p (t f) -> p t f", f=D)
                               ).then_inc(yw_stored, 16)

            def weights(g):
                pool.wait_ge(v_ready, g + 1)
                pool.tensor_tensor(r_g[:].rearrange("p a b -> p (a b)"), v_g[:].rearrange("p a b -> p (a b)"),
                                   half[:], ALU.pow).then_inc(r_ready, 1)
                pool.wait_ge(s_ready, g + 1)
                pool.tensor_copy(s_all[:, ds(g * (GT * KNN), GT * KNN)], s_g[:].rearrange("p a b -> p (a b)"))
                pool.tensor_tensor(sum_a[:], s_g[:, :, 0], s_g[:, :, 1], ALU.add).then_inc(pool_step, 1)
                pool.tensor_tensor(sum_b[:], s_g[:, :, 2], s_g[:, :, 3], ALU.add).then_inc(pool_step, 1)
                pool.wait_ge(pool_step, 5 * g + 2)
                pool.tensor_tensor(sum_a[:], sum_a[:], sum_b[:], ALU.add).then_inc(pool_step, 1)
                pool.wait_ge(pool_step, 5 * g + 3)
                pool.tensor_tensor(sum_b[:], sum_a[:], rs_all[:, ds(g * GT, GT)], ALU.add).then_inc(pool_step, 1)
                pool.wait_ge(pool_step, 5 * g + 4)
                pool.wait_ge(yw_done, g + 1)
                pool.tensor_tensor(d2_g[:], sum_b[:], neghalf[:], ALU.pow).then_inc(pool_step, 1)
                pool.wait_ge(pool_step, 5 * g + 5)
                pool.tensor_copy(d2_all[:, ds(g * GT, GT)], d2_g[:])
                pool.wait_ge(xg_loaded, 16 * (g + 1))
                pool.tensor_tensor(ystage[:], ystage[:], d2_g[:].unsqueeze(2).to_broadcast([P, GT, D]),
                                   ALU.mult).then_inc(ystage_ready, 1)

            def group(g, first=False, second=False):
                add_squares(g * GT)
                add_squares(g * GT + 1)
                if not first:
                    if not second:
                        store_table(g - 2)
                    weights(g - 1)
                with pool.Fori(2, GT) as k:
                    add_squares(g * GT + k)

            pool.wait_ge(sqb_done, NB + 2)
            group(0, first=True)
            group(1, second=True)
            with pool.Fori(2, NG) as g:
                group(g)
            store_table(NG - 2)
            weights(NG - 1)
            store_table(NG - 1)

            pool.wait_ge(gram_ready, NH * NT)
            pool.memset(eps_c[:], EPS_LN).then_inc(pool_consts, 1)
            pool.wait_ge(nb_ready, NG)
            pool.wait_ge(yw_stored, 16 * NG)
            with pool.Fori(0, (NT // 4) // 2) as half_s:
                s = half_s * 2
                for par in range(2):
                    pool.wait_ge(gsum_done, s + par + 1)
                    pool.tensor_copy(idx_c[:, par, :], nb_all[:, ds((s + par) * (4 * KNN), 4 * KNN)]
                                     ).then_inc(idx_ready, 1)
                    pool.wait_ge(idx_ready, s + par + 1)
                    apart(pool)
                    for k in range(4 * KNN):
                        pool.indirect_dma_start(
                            rows4[:, par, k, :], None, yw_table,
                            bass.IndirectOffsetOnAxis(ap=idx_c[:, par, k:k + 1], axis=0)
                        ).then_inc(gathered[par], 16)

        @block.scalar
        def _(act):
            for count in (gram_free, quarter_ready, ycur_ready):
                act.sem_inc(count, 1)
            for count in y_stored:
                act.sem_inc(count, 16)
            act.sem_inc(sqb_done, 2)
            act.wait_ge(consts_loaded, 4 * 16)

            def row1(ib, first):
                if not first:
                    act.wait_ge(p1_rows, ib + 1)
                    act.activation(aggT[:, ds(ib * BLK, BLK)], pp[:, 0, :], ACT.Copy).then_inc(agg_saved, 1)
                act.wait_ge(rowsum_ready, ib + 1)
                act.activation(rs_c[:], ps_rs[:, 0:TPB], ACT.Copy).then_inc(rs_ready, 1)
                act.activation(rs_all[:, ds(ib * TPB, TPB)], ps_rs[:, 0:TPB], ACT.Copy)
                act.wait_ge(d1_ready, ib + 1)
                for k in range(TPB):
                    ys = y1[:, ds(ib * WB // TPB + k * D, D)]
                    act.activation(ys, ys, ACT.Copy, scale=d1_c[:, k:k + 1])
                act.activation(d1_all[:, ds(ib * TPB, TPB)], d1_c[:], ACT.Copy).then_inc(y1_ready, 1)

            row1(0, True)
            with act.Fori(1, NB) as ib:
                row1(ib, False)

            act.wait_ge(rowsum_ready, NB)
            act.wait_ge(p1_rows, NB)
            with act.Fori(0, NB) as ib:
                act.wait_ge(zt_ready, ib + 2)
                act.activation(zTh[:, ds(ib * BLK, BLK)], ps_zt, ACT.Copy).then_inc(zh_done, 1)

            def stationary(t, par):
                for dst, src in ((stat_h, zTh), (stat_l, zTl)):
                    ins = act.activation(dst[:, par, :], src[:, ds(t * P, P)].bitcast(F32), ACT.Copy)
                ins.then_inc(stat_ready, 1)

            def scores(t, par, last=False):
                for h in range(NH):
                    act.wait_ge(gram_ready, t * NH + h + 1)
                    q = h // 2
                    if h % 2 == 0:
                        act.wait_ge(quarter_free, t * NQ + q + 1)
                    ins = act.activation(keys[:, q, (h % 2) * HW:(h % 2 + 1) * HW],
                                         gb[:, 2 * (h % 2):2 * (h % 2) + 2, :].rearrange("p a b -> p (a b)"),
                                         ACT.Copy)
                    ins.then_inc(gram_free, 1) if h % 2 == 0 else ins.then_inc(quarter_ready, 1)
                    if h == 0 and not last:
                        stationary(t + 1, 1 - par)

            def load_group(g):
                if not isinstance(g, int) or g > 0:
                    act.wait_ge(yw_stored, 16 * g)
                act.dma_start(xw_g[:], xT[:, ds(g * (GT * P), GT * P)]).then_inc(xtg_loaded, 16)

            def load_x(g):
                act.dma_start(ystage[:], x_t[:, ds(g * GT, GT), :]).then_inc(xg_loaded, 16)

            def exp_group(g):
                act.wait_ge(r_ready, g + 1)
                if not isinstance(g, int) or g > 0:
                    act.wait_ge(ystage_ready, g)
                act.activation(s_g[:].rearrange("p a b -> p (a b)"), r_g[:].rearrange("p a b -> p (a b)"),
                               ACT.Exp, scale=-0.5).then_inc(s_ready, 1)

            def next_rows(g, more=True):
                act.wait_ge(ystage_ready, g + 1)
                act.wait_ge(prod_ready, (g * GT + 1) * IBS)
                act.activation(ycur[:], ystage[:].rearrange("p t f -> p (t f)"), ACT.Copy).then_inc(ycur_ready, 1)
                act.wait_ge(ycur_ready, g + 2)
                if more:
                    load_x(g + 1)

            def group(g, product, first=False, last=False):
                if product:
                    next_rows(g - LAG)
                scores(g * GT, 0)
                scores(g * GT + 1, 1)
                if first:
                    load_x(0)
                else:
                    exp_group(g - 1)
                    load_group(g - 1)
                pairs = GT - 2 if not last else GT - 4
                with act.Fori(0, pairs // 2) as half_k:
                    k = half_k * 2
                    scores(g * GT + 2 + k, 0)
                    scores(g * GT + 3 + k, 1)
                if last:
                    scores(g * GT + GT - 2, 0)
                    scores(g * GT + GT - 1, 1, last=True)

            act.wait_ge(zl_done, NB)
            with act.Fori(0, NB // 2) as half_b:
                for par in range(2):
                    b = half_b * 2 + par
                    act.wait_ge(sqb_ready, b + 3)
                    act.activation(sqb[:, ds(b * BLK, BLK)], px[:, par, :], ACT.Copy).then_inc(sqb_done, 1)
            stationary(0, 0)
            group(0, False, first=True)
            group(1, False)
            with act.Fori(LAG, NG - 1) as g:
                group(g, True)
            group(NG - 1, True, last=True)
            next_rows(NG - 2)
            exp_group(NG - 1)
            load_group(NG - 1)
            next_rows(NG - 1, more=False)

            def norm_load(q, par):
                act.dma_start(xb[:, par], x_t[:, ds(q * GT, GT), :]).then_inc(xb_loaded[par], 16)

            act.wait_ge(gram_ready, NH * NT)
            act.wait_ge(pool_consts, CONSTS + 1)
            def finish(q, par, more):
                act.wait_ge(var_ready, q + 1)
                act.activation(sd[:], mv[:, :, 1], ACT.Sqrt, bias=eps_c[:]).then_inc(sd_ready, 1)
                act.wait_ge(y_ready, q + 1)
                act.dma_start(out_t[:, ds(q * GT, GT), :], y_out[:, par]).then_inc(y_stored[par], 16)
                if more:
                    norm_load(q + 2, par)

            act.dma_start(b2b[:], b2.partition_broadcast(P)).then_inc(b2_loaded, 16)
            norm_load(0, 0)
            norm_load(1, 1)
            with act.Fori(0, (GT - 2) // 2) as half_q:
                q = half_q * 2
                finish(q, 0, True)
                finish(q + 1, 1, True)
            finish(GT - 2, 0, False)
            finish(GT - 1, 1, False)
            for par in range(2):
                act.wait_ge(y_stored[par], 16 * (GT // 2 + 1))

        @block.tensor
        def _(pe):
            pe.wait_ge(pool_consts, CONSTS)

            for count in (p1_rows, z_ready, zt_ready):
                pe.sem_inc(count, 1)
            pe.sem_inc(sqb_ready, 2)

            for ib in range(NB):
                if ib >= 2:
                    pe.wait_ge(agg_saved, ib - 1)
                for jb in range(ib):
                    pe.wait_ge(loaded[jb], 16 * (ib + 1))
                    if jb == ib - 1:
                        pe.wait_ge(y1_ready, ib)
                    for jt in range(TPB):
                        mm = pe.matmul(pp[:, 0, :], y1[:, (jb * TPB + jt) * D:(jb * TPB + jt + 1) * D],
                                       ring1[:, jb, jt * BLK:(jt + 1) * BLK],
                                       start=(jb == 0 and jt == 0), stop=(jb == ib - 1 and jt == TPB - 1))
                    if jb == ib - 1:
                        mm.then_inc(p1_rows, 1)
                    elif ib == NB - 1 and jb < R2:
                        mm.then_inc(p1_tail, 1)
                pe.wait_ge(rows_added, (NB - 1) * (ib + 1))
                if ib >= 1:
                    pe.wait_ge(y1_ready, ib)
                for it in range(TPB):
                    for jt in range(TPB):
                        mm = pe.matmul(ps_rs[:, it:it + 1], acc[:, jt * BLK + it * P:jt * BLK + (it + 1) * P],
                                       ones[:, 0:1], start=(jt == 0), stop=(jt == TPB - 1))
                mm.then_inc(rowsum_ready, 1)

            def z_product(r):
                pe.wait_ge(usum_ready, r + 1)
                if r >= 1:
                    pe.wait_ge(z_done, r)
                for it in range(TPB):
                    mm = pe.matmul(ps_z[:, it * D:(it + 1) * D], usum[:, it * P:(it + 1) * P], w1[:],
                                   start=True, stop=True)
                mm.then_inc(z_ready, 1)

            def z_transpose(r):
                pe.wait_ge(z_done, r + 1)
                if r >= 1:
                    pe.wait_ge(zl_done, r)
                for it in range(TPB):
                    mm = pe.transpose(ps_zt[:, it * P:(it + 1) * P], z_c[:, it, :], ident[:])
                mm.then_inc(zt_ready, 1)

            pe.wait_ge(agg_saved, NB - 1)
            pe.wait_ge(y1_ready, NB)
            for m, (ib, jb) in enumerate(pass2):
                if jb == ib and ib >= 2:
                    pe.wait_ge(usum_ready, ib - 1)
                pe.wait_ge(loaded[m % R2], LAND1 + 16 * (m // R2 + 1))
                for jt in range(TPB):
                    mm = pe.matmul(pp[:, ib % 2, :], y1[:, (jb * TPB + jt) * D:(jb * TPB + jt + 1) * D],
                                   ring2[:, m % R2, jt * BLK:(jt + 1) * BLK],
                                   start=(jb == ib and jt == 0), stop=(jb == NB - 1 and jt == TPB - 1))
                mm.then_inc(p2_rows if jb == NB - 1 else p2_blocks, 1)
                if ib >= 1 and jb == ib:
                    z_product(ib - 1)
                if ib >= 1 and jb == min(ib + 1, NB - 1):
                    z_transpose(ib - 1)
            z_product(NB - 1)
            z_transpose(NB - 1)

            with pe.Fori(0, NB // 2) as half_b:
                for par in range(2):
                    b = half_b * 2 + par
                    pe.wait_ge(diag_ready, b + 1)
                    pe.wait_ge(sqb_done, b + 1)
                    mm = pe.matmul(px[:, par, :], ones[:], ystage[:, par * TPB:(par + 1) * TPB, :].rearrange(
                        "p a b -> p (a b)"), start=True, stop=True)
                    mm.then_inc(sqb_ready, 1)
            pe.wait_ge(zl_done, NB)
            pe.sem_inc(prod_ready, IBS)

            def scores(t, par):
                pe.wait_ge(stat_ready, t + 1)
                for h in range(NH):
                    if h % 2 == 0:
                        pe.wait_ge(gram_free, t * NQ + h // 2 + 1)
                    else:
                        pe.wait_ge(quarter_ready, t * NQ + h // 2 + 1)
                    for c in range(2):
                        bank = gb[:, 2 * (h % 2) + c, :]
                        cols = slice((2 * h + c) * BLK, (2 * h + c + 1) * BLK)
                        pe.matmul(bank, stat_h[:, par, :], zTh[:, cols], start=True, stop=False)
                        pe.matmul(bank, stat_h[:, par, :], zTl[:, cols], start=False, stop=False)
                        mm = pe.matmul(bank, stat_l[:, par, :], zTh[:, cols], start=False, stop=True)
                    mm.then_inc(gram_ready, 1)

            def product(s, c, tail=False, last=False):
                if last:
                    pe.wait_ge(ofin_ready, (s - (NG - 1) * GT - 1) * IBS + c + 1)
                else:
                    pe.wait_ge(prod_free, s * IBS + c + 1)
                for b in range(BPG):
                    i = c * BPG + b
                    a = (a_tail if tail else a_ring)[:, i if tail else i % 3, :]
                    pe.wait_ge(a_loaded[i], (s + 1) * 16)
                    for jt in range(TPB):
                        k = b * TPB + jt
                        mm = pe.matmul(pp[:, c, :], ycur[:, k * D:(k + 1) * D], a[:, jt * BLK:(jt + 1) * BLK],
                                       start=(k == 0), stop=(k == GT - 1))
                    mm.then_inc(prod_ready if b == BPG - 1 else block_used, 1)

            def x_w2(g):
                pe.wait_ge(xtg_loaded, 16 * (g + 1))
                pe.wait_ge(yw_done, g + 1)
                for k in range(GT):
                    mm = pe.matmul(px[:, k // TPB, (k % TPB) * D:(k % TPB + 1) * D], xw_g[:, k * P:(k + 1) * P],
                                   w2[:], start=True, stop=True)
                mm.then_inc(psx_ready, 1)

            with pe.Fori(0, GT // 2) as half_k:
                k = half_k * 2
                scores(k, 0)
                scores(k + 1, 1)
            with pe.Fori(0, GT // 2) as half_k:
                k = half_k * 2
                scores(k + GT, 0)
                scores(k + GT + 1, 1)
            x_w2(0)
            with pe.Fori(LAG, NG) as g:
                with pe.Fori(0, GT // 2) as half_k:
                    k = half_k * 2
                    for par in range(2):
                        scores(g * GT + k + par, par)
                        pe.wait_ge(ycur_ready, g - LAG + 2)
                        for c in range(IBS):
                            product((g - LAG) * GT + k + par, c)
                x_w2(g - 1)
            pe.wait_ge(ycur_ready, NG - LAG + 2)
            for c in range(IBS):
                product((NG - LAG) * GT, c, tail=True)
            x_w2(NG - 1)
            with pe.Fori(1, GT) as k:
                for c in range(IBS):
                    product((NG - LAG) * GT + k, c, tail=True)

            def last_product(q, par):
                pe.wait_ge(ofin_ready, IBS * (q + 1))
                pe.wait_ge(fin_step, q + 1)
                for c in range(IBS):
                    for it in range(TPB):
                        mm = pe.matmul(px[:, c, it * D:(it + 1) * D], ofin[:, par, c, it * P:(it + 1) * P],
                                       w2[:], start=True, stop=True)
                mm.then_inc(fin_ready, 1)

            end = (NG - 1) * GT
            pe.wait_ge(ycur_ready, NG + 1)
            product(end, 0, True)
            product(end, 1, True)
            product(end + 1, 0, True, True)
            last_product(0, 0)
            product(end + 1, 1, True, True)
            with pe.Fori(1, GT // 2) as half_q:
                q = half_q * 2
                for par in range(2):
                    product(q + end + par, 0, True, True)
                    last_product(q + par - 1, 1 - par)
                    product(q + end + par, 1, True, True)
            last_product(GT - 1, 1)

        @block.vector
        def _(dve):
            dve.sem_inc(yw_done, 1)

            def add_row(ib, first):
                for jb in range(1, NB):
                    if jb == 1:
                        dve.wait_ge(loaded[0], (ib + 1) * 16)
                        if not first:
                            dve.wait_ge(rowsum_ready, ib)
                    else:
                        dve.wait_ge(rows_added, ib * (NB - 1) + jb - 1)
                    dve.wait_ge(loaded[jb], (ib + 1) * 16)
                    dve.tensor_tensor(acc[:], ring1[:, 0, :] if jb == 1 else acc[:], ring1[:, jb, :],
                                      ALU.add).then_inc(rows_added, 1)

            add_row(0, True)
            with dve.Fori(1, NB) as ib:
                add_row(ib, False)

            dve.wait_ge(agg_zeroed, 1)
            dve.wait_ge(p1_rows, NB)
            dve.wait_ge(consts_loaded, 4 * 16)
            with dve.Fori(0, NB // 2) as half_two:
                two = half_two * 2
                for par in range(2):
                    ib = two + par
                    at = 7 * ib
                    dve.wait_ge(p2_rows, ib + 1)
                    dve.wait_ge(z_ready, ib + 1)
                    dve.tensor_tensor(usum[:], pp[:, par, :], aggT[:, ds(ib * BLK, BLK)],
                                      ALU.add).then_inc(usum_ready, 1)
                    dve.tensor_copy(d1_z[:], d1_all[:, ds(ib * TPB, TPB)]).then_inc(zstep, 1)
                    dve.wait_ge(zstep, at + 1)
                    dve.wait_ge(z_ready, ib + 2)
                    dve.wait_ge(zt_ready, ib + 1)
                    for it in range(TPB):
                        dve.scalar_tensor_tensor(out=z_c[:, it, :], in0=ps_z[:, it * D:(it + 1) * D],
                                                 scalar=d1_z[:, it:it + 1], in1=b1b[:], op0=ALU.mult,
                                                 op1=ALU.add).then_inc(zstep, 1)
                    zf = z_c[:].rearrange("p a b -> p (a b)")
                    dve.wait_ge(zstep, at + 5)
                    dve.scalar_tensor_tensor(out=zf, in0=zf, scalar=0.1, in1=zf, op0=ALU.mult,
                                             op1=ALU.max).then_inc(zstep, 1)
                    dve.wait_ge(zstep, at + 6)
                    for it in range(TPB):
                        ins = dve.tensor_tensor_reduce(out=junk[:, it, :], in0=z_c[:, it, :], in1=z_c[:, it, :],
                                                       scale=1.0, scalar=0.0, op0=ALU.mult, op1=ALU.add,
                                                       accum_out=sq_c[:, it:it + 1])
                    ins.then_inc(zstep, 1)
                    dve.wait_ge(zstep, at + 7)
                    dve.tensor_copy(sq_all[:, ds(ib * TPB, TPB)], sq_c[:]).then_inc(z_done, 1)
                    dve.wait_ge(zh_done, ib + 1)
                    cols = ds(ib * BLK, BLK)
                    dve.tensor_tensor(zTl[:, cols], ps_zt, zTh[:, cols].bitcast(F32),
                                      ALU.subtract).then_inc(zl_done, 1)

            dve.wait_ge(p2_rows, NB)
            with dve.Fori(0, NB // 2) as half_b:
                for par in range(2):
                    b = half_b * 2 + par
                    dve.wait_ge(sqb_ready, b + 1)
                    dve.tensor_copy(sq_c4[:, par, :], sq_all[:, ds(b * TPB, TPB)]).then_inc(sq_step, 1)
                    dve.wait_ge(sq_step, b + 1)
                    for k in range(TPB):
                        ins = dve.tensor_scalar(ystage[:, par * TPB + k, :], ident[:], sq_c4[:, par, k:k + 1],
                                                -0.5, ALU.mult, ALU.mult)
                    ins.then_inc(diag_ready, 1)
            dve.sem_inc(quarter_free, NQ)
            dve.sem_inc(prod_free, IBS)

            def neighbours(g, k):
                at = (g * GT + k) * (NQ + 1)
                for q in range(NQ):
                    dve.wait_ge(quarter_keyed, (g * GT + k) * NQ + q + 1)
                    c8 = cand[:, k % 2, q * TOP:(q + 1) * TOP]
                    apart(dve)
                    dve.max(c8, keys[:, q, :]).then_inc(knn_step, 1)
                    dve.wait_ge(knn_step, at + q + 1)
                    apart(dve)
                    dve.max_index(cand_at[:, k, q * TOP:(q + 1) * TOP], c8, keys[:, q, :]
                                  ).then_inc(quarter_free, 1)
                dve.max(topv[:, k, :], cand[:, k % 2, :]).then_inc(knn_step, 1)
                dve.wait_ge(knn_step, at + NQ + 1)
                apart(dve)
                dve.max_index(top_at[:, k, :], topv[:, k, :], cand[:, k % 2, :])

            def add_product(s, q, c):
                dve.wait_ge(prod_ready, s * IBS + c + 1 + IBS)
                cols = q * IBS * BLK + c * BLK
                cols = ds(cols, BLK) if not isinstance(cols, int) else slice(cols, cols + BLK)
                dve.tensor_tensor(aggT[:, cols], aggT[:, cols], pp[:, c, :], ALU.add).then_inc(prod_free, 1)

            def distances(g):
                at = g * 16
                if not isinstance(g, int) or g > 0:
                    dve.wait_ge(r_ready, g)
                dve.wait_ge(knn_step, (g * GT + GT) * (NQ + 1))
                sq = sq_all[:, ds(g * GT, GT)].unsqueeze(2).to_broadcast([P, GT, KNN])
                dve.scalar_tensor_tensor(out=v_g[:], in0=topv[:, :, 0:KNN], scalar=-2.0, in1=sq,
                                         op0=ALU.mult, op1=ALU.add).then_inc(grp_step, 1)
                dve.wait_ge(grp_step, at + 1)
                dve.tensor_scalar(v_g[:], v_g[:], 0.0, EPS_D2, ALU.max, ALU.add).then_inc(v_ready, 1)
                dve.tensor_copy(top_f[:], top_at[:, :, 0:KNN]).then_inc(grp_step, 1)
                dve.tensor_copy(cand_f, cand_at[:]).then_inc(grp_step, 1)
                dve.wait_ge(grp_step, at + 3)
                dve.tensor_tensor(cand_f, cand_f, quarter_at[:].unsqueeze(1).to_broadcast([P, GT, NC]),
                                  ALU.add).then_inc(grp_step, 1)
                dve.wait_ge(grp_step, at + 4)
                for k in range(KNN):
                    if k:
                        dve.wait_ge(grp_step, at + 4 + 3 * k)
                    dve.tensor_tensor(pick[:], iota_c[:].unsqueeze(1).to_broadcast([P, GT, NC]),
                                      top_f[:, :, k:k + 1].to_broadcast([P, GT, NC]), ALU.is_equal
                                      ).then_inc(grp_step, 1)
                    dve.wait_ge(grp_step, at + 5 + 3 * k)
                    dve.tensor_tensor(pick[:], pick[:], cand_f, ALU.mult).then_inc(grp_step, 1)
                    dve.wait_ge(grp_step, at + 6 + 3 * k)
                    dve.tensor_reduce(nb_f[:, :, k], pick[:], AX_X, ALU.add).then_inc(grp_step, 1)
                dve.wait_ge(grp_step, at + 16)
                dve.tensor_copy(nb_all[:, ds(g * (GT * KNN), GT * KNN)], nb_f[:].rearrange("p a b -> p (a b)")
                                ).then_inc(nb_ready, 1)

            def table_rows(g):
                dve.wait_ge(psx_ready, g + 1)
                dve.wait_ge(ystage_ready, g + 1)
                for c in range(2):
                    ins = dve.tensor_tensor(
                        xw_g[:, c * BLK:(c + 1) * BLK].rearrange("p (t f) -> p t f", f=D),
                        px[:, c, :].rearrange("p (t f) -> p t f", f=D),
                        d2_g[:, c * TPB:(c + 1) * TPB].unsqueeze(2).to_broadcast([P, TPB, D]), ALU.mult)
                ins.then_inc(yw_done, 1)

            def group(g, product):
                for k in range(GT):
                    neighbours(g, k)
                    if product:
                        for c in range(IBS):
                            add_product((g - LAG) * GT + k, k, c)
                distances(g)

            dve.wait_ge(pool_consts, CONSTS)
            group(0, False)
            group(1, False)
            table_rows(0)
            dve.wait_ge(agg_zeroed, 2)
            with dve.Fori(LAG, NG) as g:
                group(g, True)
                table_rows(g - 1)

            dve.wait_ge(gram_ready, NH * NT)
            dve.sem_inc(gsum_done, 2)

            def sum_neighbours(s, par):
                dve.tensor_copy(s_c[:, par, :], s_all[:, ds(s * (4 * KNN), 4 * KNN)]).then_inc(scal_ready, 1)
                dve.wait_ge(scal_ready, s + 1)
                dve.wait_ge(gathered[par], (s - par) * (4 * KNN * 8) + 16 * 4 * KNN)
                for k in range(KNN):
                    if k:
                        dve.wait_ge(gs_step, s * 3 + k)
                    for i in range(4):
                        to = gsum[:, ds(s * (4 * D) + i * D, D)]
                        j = i * KNN + k
                        if k == 0:
                            ins = dve.tensor_scalar(to, rows4[:, par, j, :], s_c[:, par, j:j + 1], None, ALU.mult)
                        else:
                            ins = dve.scalar_tensor_tensor(out=to, in0=rows4[:, par, j, :],
                                                           scalar=s_c[:, par, j:j + 1], in1=to,
                                                           op0=ALU.mult, op1=ALU.add)
                    ins.then_inc(gsum_done if k == KNN - 1 else gs_step, 1)

            s0 = (NG - LAG) * GT
            add_product(s0, 0, 0)
            add_product(s0, 0, 1)
            table_rows(NG - 1)
            dve.wait_ge(yw_done, NG + 1)
            dve.sem_inc(fin_step, 1)
            sum_neighbours(0, 0)
            add_product(s0 + 1, 1, 0)
            add_product(s0 + 1, 1, 1)
            sum_neighbours(1, 1)
            with dve.Fori(1, GT // 2) as half_q:
                q = half_q * 2
                for par in range(2):
                    add_product(q + s0 + par, q + par, 0)
                    add_product(q + s0 + par, q + par, 1)
                    sum_neighbours(q + par, par)

            def complete(q, par):
                for c in range(IBS):
                    dve.wait_ge(prod_ready, (q + (NG - 1) * GT) * IBS + c + 1 + IBS)
                    dve.tensor_tensor(ofin[:, par, c, :], aggT[:, ds(q * (IBS * BLK) + c * BLK, BLK)],
                                      pp[:, c, :], ALU.add).then_inc(ofin_ready, 1)

            def norm(q, par):
                at = q * 5
                dve.wait_ge(fin_ready, q + 1)
                dve.wait_ge(gsum_done, 2 * q + 4)
                if not isinstance(q, int) or q > 0:
                    dve.wait_ge(y_ready, q)
                for c in range(IBS):
                    ins = dve.tensor_tensor(res[:, c * TPB:(c + 1) * TPB, :].rearrange("p t f -> p (t f)"),
                                            px[:, c, :], gsum[:, ds(q * (GT * D) + c * BLK, BLK)], ALU.add)
                ins.then_inc(fin_step, 1)
                dve.tensor_copy(d2_f[:], d2_all[:, ds(q * GT, GT)]).then_inc(norm_step, 1)
                if isinstance(q, int) and q == 0:
                    dve.wait_ge(b2_loaded, 16)
                dve.wait_ge(xb_loaded[par], (q - par) * 8 + 16)
                dve.tensor_tensor(xb[:, par], xb[:, par], b2b[:].unsqueeze(1).to_broadcast([P, GT, D]),
                                  ALU.add).then_inc(norm_step, 1)
                dve.wait_ge(fin_step, q + 2)
                dve.wait_ge(norm_step, at + 2)
                for i in range(GT):
                    ins = dve.scalar_tensor_tensor(out=res[:, i, :], in0=res[:, i, :], scalar=d2_f[:, i:i + 1],
                                                   in1=xb[:, par, i, :], op0=ALU.mult, op1=ALU.add)
                ins.then_inc(norm_step, 1)
                dve.wait_ge(norm_step, at + 3)
                for i in range(GT):
                    ins = dve.bn_stats(stats[:, i, :], res[:, i, :])
                ins.then_inc(norm_step, 1)
                dve.wait_ge(norm_step, at + 4)
                apart(dve)
                for i in range(GT):
                    ins = dve.bn_aggr(mv[:, i, :], stats[:, i, :])
                ins.then_inc(var_ready, 1)
                dve.wait_ge(sd_ready, q + 1)
                dve.reciprocal(rstd[:], sd[:]).then_inc(norm_step, 1)
                dve.wait_ge(norm_step, at + 5)
                dve.wait_ge(y_stored[par], (q - par) * 8 + 16)
                for i in range(GT):
                    ins = dve.tensor_scalar(y_out[:, par, i, :], res[:, i, :], mv[:, i, 0:1], rstd[:, i:i + 1],
                                            ALU.subtract, ALU.mult)
                ins.then_inc(y_ready, 1)

            complete(0, 0)
            sum_neighbours(GT, 0)
            complete(1, 1)
            sum_neighbours(GT + 1, 1)
            norm(0, 0)
            with dve.Fori(1, GT // 2) as half_q:
                q = half_q * 2
                for par in range(2):
                    complete(q + par, par)
                    sum_neighbours(q + (GT + par), par)
                    norm(q + (par - 1), 1 - par)
            norm(GT - 1, 1)


def kernel(x, adj, L0_gnn_W1, L0_gnn_b1, L0_gnn_W2, L0_gnn_b2):
    import numpy as np
    import concourse.bacc as bacc
    from concourse.bass_utils import run_bass_kernel_spmd

    x, adj = np.asarray(x), np.asarray(adj)
    nb = adj.shape[0] // BLK
    arrays = {
        "x": np.ascontiguousarray(x),
        "xT": np.ascontiguousarray(x.T),
        "adjb": np.ascontiguousarray(
            adj.reshape(nb, BLK, nb, TPB, P).transpose(0, 2, 4, 3, 1)).reshape(nb, nb, P, TPB * BLK),
        "W1": np.ascontiguousarray(L0_gnn_W1), "b1": np.ascontiguousarray(L0_gnn_b1),
        "W2": np.ascontiguousarray(L0_gnn_W2), "b2": np.ascontiguousarray(L0_gnn_b2),
    }
    nc = bacc.Bacc("TRN2", target_bir_lowering=False, num_devices=1)
    args = {n: nc.dram_tensor(n, a.shape, mybir.dt.from_np(a.dtype), kind="ExternalInput").ap()
            for n, a in arrays.items()}
    args["out"] = nc.dram_tensor("out", x.shape, F32, kind="ExternalOutput").ap()
    gnn_resnorm(nc, **args)
    r = run_bass_kernel_spmd(nc, [arrays], core_ids=[0])
    return r.results[0]["out"]
```

```python
from contextlib import ExitStack

import concourse.bass as bass
from concourse import mybir

F32 = mybir.dt.float32
F32R = mybir.dt.float32r
U32 = mybir.dt.uint32
I32 = mybir.dt.int32
ALU = mybir.AluOpType
ACT = mybir.ActivationFunctionType
AX_X = mybir.AxisListType.X

P = 128
BLK = 512
TPB = BLK // P
GT = 8
KNN = 4
TOP = 8
KEEP = 3
BANKS1 = 6
LAG = 20
EPS_D2 = 1e-10
EPS_LN = 1e-5
ds = bass.ds


def gnn_resnorm(nc, x, xT, adjb, W1, b1, W2, b2, out):
    N, D = x.shape
    NT = N // P
    NB = N // BLK
    NG = NT // GT
    BPG = GT // TPB
    IBS = NB // GT
    QW = 2048
    NQ = N // QW
    HW = 2 * BLK
    NH = N // HW
    MID = NT - LAG
    NC = NQ * TOP
    STREAM = 8
    PER_ROW = NB - KEEP
    LONE = NB - 1 - KEEP
    R2 = 4
    WB = TPB * BLK
    assert D == P and IBS == 2 and NB == 16 and LAG == 5 * GT // 2 and LONE % BANKS1 == 0
    assert (NB - LONE) * BLK == WB and R2 < STREAM

    def columns(r):
        return [(r + KEEP + 1 + k) % NB for k in range(NB)]

    kept_slots = [STREAM + sum(e + 1 for e in range(1, d)) for d in range(1, KEEP + 2)]
    SLOTS1 = kept_slots[KEEP]

    def slot1(r, k):
        if k < PER_ROW:
            use, slot = divmod(r * PER_ROW + k, STREAM)
        else:
            d = k - PER_ROW + 1
            use, at = divmod(r, d + 1)
            slot = kept_slots[d - 1] + at
        return slot, use

    def held_before(slot, use):
        if slot < STREAM:
            return divmod((use - 1) * STREAM + slot, PER_ROW)
        d = max(e for e in range(1, KEEP + 1) if kept_slots[e - 1] <= slot)
        return (use - 1) * (d + 1) + slot - kept_slots[d - 1], PER_ROW + d - 1

    WAITED_AT = (2.5, 4.5, 6.5, 8.5)
    pass1 = []
    for r in range(NB):
        turns = [(k, r, jb) for k, jb in enumerate(columns(r)) if jb < r]
        turns += [(WAITED_AT[d], r - 1 - d, r - 1) for d in range(min(KEEP + 1, r))]
        pass1 += [(c, jb) for _, c, jb in sorted(turns)] + [(r, None)]
    pass1 += [(c, NB - 1) for c in range(NB - 1 - KEEP, NB)]
    last_of = [min(r + KEEP, NB - 1) for r in range(NB)]
    done1 = {}
    counts = [0, 0]
    for r, jb in pass1:
        if jb is not None:
            completes = jb == last_of[r]
            counts[completes] += 1
            done1[r, jb] = completes, counts[completes]

    x_t = x.rearrange("(t p) f -> p t f", p=P)
    out_t = out.rearrange("(t p) f -> p t f", p=P)
    yw_table = nc.dram_tensor("yw_table", (N, D), F32, kind="Internal").ap()
    yw_t = yw_table.rearrange("(t p) f -> p t f", p=P)

    whole = ExitStack()
    with whole:
        def maker(stack):
            return lambda name, shape, dt=F32, side=None: stack.enter_context(
                nc.sbuf_tensor(name, shape, dt, **({"side": side} if side else {})))

        def sem(name):
            return whole.enter_context(nc.semaphore(name))

        def psum(name, shape):
            return whole.enter_context(nc.psum_tensor(name, shape, F32))

        sb = maker(whole)
        aggT = sb("aggT", [P, N])
        y1 = sb("y1", [P, NT * D])
        w1 = sb("w1", [P, D])
        w2 = sb("w2", [P, D])
        b1b = sb("b1b", [P, D])
        ident = sb("ident", [P, P])
        ones = sb("ones", [P, P])
        neghalf = sb("neghalf", [P, GT])
        iota_c = sb("iota_c", [P, NC])
        quarter_at = sb("quarter_at", [P, NC])
        rs_all = sb("rs_all", [P, NT])
        d1_all = sb("d1_all", [P, NT])
        d2_all = sb("d2_all", [P, NT])
        sq_all = sb("sq_all", [P, NT])
        s_all = sb("s_all", [P, NT * KNN])
        nb_all = sb("nb_all", [P, NT * KNN], U32)
        rs_c = sb("rs_c", [P, TPB])
        d1_c = sb("d1_c", [P, TPB])

        gb = psum("gb", [P, 4, BLK])
        pp = psum("pp", [P, 2, IBS, BLK])
        px = pp[:, 1]
        ps_rs, ps_z, ps_zt = (gb[:, k, :] for k in range(3))
        banks1 = [px[:, 0, :], px[:, 1, :], gb[:, 3, :], pp[:, 0, 1, :], gb[:, 1, :], gb[:, 2, :]]

        consts_loaded = sem("consts_loaded")
        pool_consts = sem("pool_consts")
        wait_carrier = sem("wait_carrier")
        agg_zeroed = sem("agg_zeroed")
        loaded = [sem(f"loaded{k}") for k in range(SLOTS1)]
        rows_added = sem("rows_added")
        acc_folded = sem("acc_folded")
        p1_rows = sem("p1_rows")
        p1_blocks = sem("p1_blocks")
        rowsum_ready = sem("rowsum_ready")
        rs_ready = sem("rs_ready")
        d1_ready = sem("d1_ready")
        y1_ready = sem("y1_ready")
        agg_saved = sem("agg_saved")
        p2_blocks = sem("p2_blocks")
        p2_rows = sem("p2_rows")
        usum_ready = sem("usum_ready")
        z_ready = sem("z_ready")
        zstep = sem("zstep")
        z_done = sem("z_done")
        zt_ready = sem("zt_ready")
        zh_done = sem("zh_done")
        zl_done = sem("zl_done")
        zsq_ready = sem("zsq_ready")
        sqb_ready = sem("sqb_ready")
        sqb_done = sem("sqb_done")
        stat_ready = sem("stat_ready")
        gram_free = sem("gram_free")
        gram_ready = sem("gram_ready")
        quarter_ready = sem("quarter_ready")
        quarter_keyed = sem("quarter_keyed")
        quarter_free = sem("quarter_free")
        knn_step = sem("knn_step")
        top_ready = sem("top_ready")
        grp_step = sem("grp_step")
        v_ready = sem("v_ready")
        r_ready = sem("r_ready")
        s_ready = sem("s_ready")
        pool_step = sem("pool_step")
        d2_ready = sem("d2_ready")
        ystage_ready = sem("ystage_ready")
        ycur_ready = sem("ycur_ready")
        nb_ready = sem("nb_ready")
        xg_loaded = sem("xg_loaded")
        xtg_loaded = sem("xtg_loaded")
        psx_ready = sem("psx_ready")
        yw_done = sem("yw_done")
        yw_stored = sem("yw_stored")
        a_loaded = [sem(f"a_loaded{k}") for k in range(IBS * BPG)]
        block_used = sem("block_used")
        prod_ready = sem("prod_ready")
        prod_free = sem("prod_free")
        idx_ready = sem("idx_ready")
        gathered = [sem(f"gathered{k}") for k in range(2)]
        scal_ready = sem("scal_ready")
        gs_step = sem("gs_step")
        gsum_done = sem("gsum_done")
        ofin_ready = sem("ofin_ready")
        fin_ready = sem("fin_ready")
        fin_step = sem("fin_step")
        norm_step = sem("norm_step")
        xb_loaded = [sem(f"xb_loaded{k}") for k in range(2)]
        b2_loaded = sem("b2_loaded")
        var_ready = sem("var_ready")
        sd_ready = sem("sd_ready")
        y_ready = sem("y_ready")
        y_stored = [sem(f"y_stored{k}") for k in range(2)]

        scope = ExitStack()
        s1 = maker(scope)
        ring1 = s1("ring1", [P, SLOTS1 - 1, WB])
        slots1 = [ring1[:, k, :] for k in range(STREAM - 1)] + [aggT[:, LONE * BLK:]]
        slots1 += [ring1[:, k, :] for k in range(STREAM - 1, SLOTS1 - 1)]
        acc = s1("acc", [P, WB])
        scope.close()

        right = ExitStack()
        sr = maker(right)
        zTh = sr("zTh", [P, N], F32R, "right")
        zTl = sr("zTl", [P, N], F32R, "right")
        sqb = sr("sqb", [P, N], F32, "right")
        scope = ExitStack()
        s2 = maker(scope)
        ring2 = s2("ring2", [P, R2, WB])
        usum = s2("usum", [P, BLK])
        z_c = s2("z_c", [P, TPB, D])
        junk = s2("junk", [P, TPB, D])
        zsq = s2("zsq", [P, BLK])
        d1_z = s2("d1_z", [P, TPB])
        sq_c = s2("sq_c", [P, TPB])
        scope.close()

        scope = ExitStack()
        s3 = maker(scope)
        keys = y1[:, :].rearrange("p (s w) -> p s w", w=QW)
        a_ring = s3("a_ring", [P, 3, WB])
        ycur = s3("ycur", [P, GT * D])
        ystage = s3("ystage", [P, GT, D])
        xw_g = s3("xw_g", [P, GT * D])
        stat_h = s3("stat_h", [P, 2, P], F32R)
        stat_l = s3("stat_l", [P, 2, P], F32R)
        cand = s3("cand", [P, 2, NC])
        cand_at = s3("cand_at", [P, GT, NC], U32)
        cand_f = s3("cand_f", [P, GT, NC])
        pick = s3("pick", [P, GT, NC])
        topv = s3("topv", [P, GT, TOP])
        top_at = s3("top_at", [P, GT, TOP], U32)
        top_f = s3("top_f", [P, GT, KNN])
        nb_f = s3("nb_f", [P, GT, KNN])
        GK = GT * KNN
        v_g, r_g, s_g = (b1b[:, k * GK:(k + 1) * GK].rearrange("p (a b) -> p a b", b=KNN) for k in range(3))
        sum_a, sum_b, d2_g = (b1b[:, 3 * GK + k * GT:3 * GK + (k + 1) * GT] for k in range(3))

        right.close()
        right = ExitStack()
        sr = maker(right)
        gsum = y1
        a_tail = sr("a_tail", [P, IBS * BPG, WB], F32, "right")
        rows4 = sr("rows4", [P, 2, 4 * KNN, D], F32, "right")
        xt_last = sr("xt_last", [P, GT * P], F32, "right")
        ofin = sr("ofin", [P, 2, IBS, BLK], F32, "right")
        b2b = sr("b2b", [P, D], F32, "right")
        idx_c = sr("idx_c", [P, 2, 4 * KNN], U32, "right")
        s_c = sr("s_c", [P, 2, 4 * KNN], F32, "right")
        d2_f = sr("d2_f", [P, GT], F32, "right")
        stats = sr("stats", [P, GT, 6], F32, "right")
        mv = sr("mv", [P, GT, 2], F32, "right")
        sd = sr("sd", [P, GT], F32, "right")
        rstd = sr("rstd", [P, GT], F32, "right")
        eps_c = sr("eps_c", [P, 1], F32, "right")
        xb = sr("xb", [P, 2, GT, D], F32, "right")
        res = sr("res", [P, GT, D], F32, "right")
        y_out = sr("y_out", [P, 2, GT, D], F32, "right")
        right.close()
        scope.close()

        block = whole.enter_context(nc.Block())

        def apart(eng):
            eng.sem_inc(wait_carrier, 1)

        A_SLOTS = (0, 1, 2, 1)
        CONSTS = 8
        rows2 = [i // 2 + (i % 2) * (LONE // 2) for i in range(LONE)]
        pass2 = [(i, ib, jb) for i, ib in enumerate(rows2) for jb in range(ib + KEEP + 1, NB)]

        def uses1(slot):
            return len(range(slot, NB * PER_ROW, STREAM))

        @block.sync
        def _(sp):
            for dst, src in ((w1, W1), (w2, W2)):
                sp.dma_start(dst[:], src).then_inc(consts_loaded, 16)
            sp.dma_start(b1b[:], b1.partition_broadcast(P)).then_inc(consts_loaded, 16)

            def slot_free(slot, use):
                r, k = held_before(slot, use)
                sp.wait_ge(rows_added, (NB - 1) * r + max(k, 1))
                if (r, columns(r)[k]) in done1:
                    completes, count = done1[r, columns(r)[k]]
                    sp.wait_ge(p1_rows if completes else p1_blocks, count)

            for r in range(NB):
                for k, jb in enumerate(columns(r)):
                    slot, use = slot1(r, k)
                    if use:
                        slot_free(slot, use)
                    sp.dma_start(slots1[slot], adjb[r, jb]).then_inc(loaded[slot], 16)
                    if r == 0 and k == 0:
                        sp.dma_start(y1[:].rearrange("p (t f) -> p t f", f=D), x_t).then_inc(consts_loaded, 16)

            for m, (_, ib, jb) in enumerate(pass2):
                if m < R2:
                    slot_free(m, uses1(m))
                else:
                    was, _, was_jb = pass2[m - R2]
                    if was_jb == NB - 1:
                        sp.wait_ge(p2_rows, was + 1)
                    else:
                        sp.wait_ge(p2_blocks, m - R2 + 1 - was)
                sp.dma_start(ring2[:, m % R2, :], adjb[ib, jb]).then_inc(loaded[m % R2], 16)

            def load_a(g, q, ring, slots):
                s = g * GT + q
                for i in range(IBS * BPG):
                    c, b = divmod(i, BPG)
                    if b == 0:
                        sp.wait_ge(block_used, s * IBS + c + 1)
                    elif slots[i] == i and slots.count(i) == 1:
                        sp.wait_ge(prod_ready, s * IBS + c + 1)
                    elif i == 1:
                        sp.wait_ge(prod_ready, s * IBS + IBS)
                    else:
                        sp.wait_ge(prod_ready, s * IBS + 1 + IBS)
                    sp.dma_start(ring[:, slots[i], :], adjb[q * IBS + c, g * BPG + b]).then_inc(a_loaded[i], 16)

            sp.wait_ge(p2_rows, LONE)
            sp.wait_ge(zl_done, NB)
            with sp.Fori(0, MID // GT) as g:
                with sp.Fori(0, GT) as q:
                    load_a(g, q, a_ring, A_SLOTS)
            with sp.Fori(0, MID % GT) as q:
                load_a(MID // GT, q, a_ring, A_SLOTS)
            sp.wait_ge(gram_ready, NH * NT)
            with sp.Fori(MID % GT, GT) as q:
                load_a(MID // GT, q, a_tail, (0, 1, 2, 3))
            with sp.Fori(MID // GT + 1, NG) as g:
                with sp.Fori(0, GT) as q:
                    load_a(g, q, a_tail, (0, 1, 2, 3))

        @block.gpsimd
        def _(pool):
            n = [0]

            def made(ins):
                n[0] += 1
                ins.then_inc(pool_consts, 1)

            made(pool.memset(ident[:], 0.0))
            made(pool.memset(ones[:], 1.0))
            made(pool.memset(neghalf[:], -0.5))
            iota_i = nb_all[:, 0:2 * NC].bitcast(I32)
            made(pool.iota(iota_i[:, 0:NC], pattern=[[1, NC]], base=0, channel_multiplier=0))
            made(pool.iota(iota_i[:, NC:2 * NC], pattern=[[QW, NQ], [0, TOP]], base=0, channel_multiplier=0))
            pool.wait_ge(pool_consts, n[0])
            made(pool.tensor_copy(iota_c[:], iota_i[:, 0:NC]))
            made(pool.tensor_copy(quarter_at[:], iota_i[:, NC:2 * NC]))
            made(pool.affine_select(out=ident[:], in_=ident[:], compare_op=ALU.not_equal, fill=1.0, base=0,
                                    pattern=[[-1, P]], channel_multiplier=1))
            assert n[0] == CONSTS

            with pool.Fori(0, NB) as ib:
                pool.wait_ge(rs_ready, ib + 1)
                pool.tensor_tensor(d1_c[:], rs_c[:], neghalf[:, 0:TPB], ALU.pow).then_inc(d1_ready, 1)

            pool.wait_ge(usum_ready, NB)
            pool.memset(aggT[:], 0.0).then_inc(agg_zeroed, 1)

            def add_squares(t):
                for q in range(NQ):
                    pool.wait_ge(quarter_ready, t * NQ + q + 2)
                    pool.tensor_tensor(keys[:, q, :], keys[:, q, :], sqb[:, q * QW:(q + 1) * QW], ALU.add
                                       ).then_inc(quarter_keyed, 1)

            def store_table(g):
                pool.wait_ge(yw_done, g + 2)
                pool.dma_start(yw_t[:, ds(g * GT, GT), :], xw_g[:].rearrange("p (t f) -> p t f", f=D)
                               ).then_inc(yw_stored, 16)

            def row_weights(g):
                pool.wait_ge(s_ready, g + 1)
                pool.tensor_copy(s_all[:, ds(g * (GT * KNN), GT * KNN)], s_g[:].rearrange("p a b -> p (a b)"))
                pool.tensor_tensor(sum_a[:], s_g[:, :, 0], s_g[:, :, 1], ALU.add).then_inc(pool_step, 1)
                pool.tensor_tensor(sum_b[:], s_g[:, :, 2], s_g[:, :, 3], ALU.add).then_inc(pool_step, 1)
                pool.wait_ge(pool_step, 5 * g + 2)
                pool.tensor_tensor(sum_a[:], sum_a[:], sum_b[:], ALU.add).then_inc(pool_step, 1)
                pool.wait_ge(pool_step, 5 * g + 3)
                pool.tensor_tensor(sum_b[:], sum_a[:], rs_all[:, ds(g * GT, GT)], ALU.add).then_inc(pool_step, 1)
                pool.wait_ge(pool_step, 5 * g + 4)
                pool.wait_ge(yw_done, g + 1)
                pool.tensor_tensor(d2_g[:], sum_b[:], neghalf[:], ALU.pow).then_inc(pool_step, 1)
                pool.wait_ge(pool_step, 5 * g + 5)
                pool.tensor_copy(d2_all[:, ds(g * GT, GT)], d2_g[:]).then_inc(d2_ready, 1)

            def scaled_rows(g):
                pool.wait_ge(xg_loaded, 16 * (g + 1))
                pool.tensor_tensor(ystage[:], ystage[:], d2_g[:].unsqueeze(2).to_broadcast([P, GT, D]),
                                   ALU.mult).then_inc(ystage_ready, 1)

            def group(g, first=False):
                with pool.Fori(0, 3) as k:
                    add_squares(g * GT + k)
                if not first:
                    row_weights(g - 1)
                with pool.Fori(3, 6) as k:
                    add_squares(g * GT + k)
                if not first:
                    scaled_rows(g - 1)
                add_squares(g * GT + 6)
                add_squares(g * GT + 7)
                if not first:
                    store_table(g - 1)

            pool.wait_ge(sqb_done, NB)
            group(0, first=True)
            with pool.Fori(1, NG) as g:
                group(g)
            row_weights(NG - 1)
            store_table(NG - 1)

            pool.wait_ge(gram_ready, NH * NT)
            pool.memset(eps_c[:], EPS_LN).then_inc(pool_consts, 1)
            pool.wait_ge(nb_ready, NG)
            pool.wait_ge(yw_stored, 16 * NG)
            with pool.Fori(0, (NT // 4) // 2) as half_s:
                s = half_s * 2
                for par in range(2):
                    pool.wait_ge(gsum_done, s + par + 1)
                    pool.tensor_copy(idx_c[:, par, :], nb_all[:, ds((s + par) * (4 * KNN), 4 * KNN)]
                                     ).then_inc(idx_ready, 1)
                    pool.wait_ge(idx_ready, s + par + 1)
                    apart(pool)
                    for k in range(4 * KNN):
                        pool.indirect_dma_start(
                            rows4[:, par, k, :], None, yw_table,
                            bass.IndirectOffsetOnAxis(ap=idx_c[:, par, k:k + 1], axis=0)
                        ).then_inc(gathered[par], 16)

        @block.scalar
        def _(act):
            for count in (gram_free, quarter_ready, ycur_ready):
                act.sem_inc(count, 1)
            for count in y_stored:
                act.sem_inc(count, 16)
            act.wait_ge(consts_loaded, 4 * 16)

            def row1(ib):
                act.wait_ge(rowsum_ready, ib + 1)
                act.activation(rs_c[:], ps_rs[:, 0:TPB], ACT.Copy).then_inc(rs_ready, 1)
                act.activation(rs_all[:, ds(ib * TPB, TPB)], ps_rs[:, 0:TPB], ACT.Copy)
                act.wait_ge(d1_ready, ib + 1)
                for k in range(TPB):
                    ys = y1[:, ds(ib * WB // TPB + k * D, D)]
                    act.activation(ys, ys, ACT.Copy, scale=d1_c[:, k:k + 1])
                act.activation(d1_all[:, ds(ib * TPB, TPB)], d1_c[:], ACT.Copy).then_inc(y1_ready, 1)

            with act.Fori(0, KEEP + 1) as ib:
                row1(ib)
            with act.Fori(0, LONE // BANKS1) as six:
                for k in range(BANKS1):
                    saved = six * BANKS1 + k
                    act.wait_ge(p1_rows, saved + 1)
                    act.activation(aggT[:, ds(saved * BLK, BLK)], banks1[k], ACT.Copy).then_inc(agg_saved, 1)
                    row1(saved + (KEEP + 1))

            act.wait_ge(rowsum_ready, NB)
            act.wait_ge(p1_rows, NB)

            def high_part(v, ib, par):
                act.wait_ge(zt_ready, v + 2)
                act.activation(zsq[:], ps_zt, ACT.Square).then_inc(zsq_ready, 1)
                act.activation(zTh[:, ds(ib * BLK, BLK)], ps_zt, ACT.Copy).then_inc(zh_done, 1)
                act.wait_ge(sqb_ready, v + 1)
                act.activation(sqb[:, ds(ib * BLK, BLK)], px[:, par, :], ACT.Copy, scale=-0.5).then_inc(sqb_done, 1)

            with act.Fori(0, (NB - LONE) // 2) as half_v:
                for par in range(2):
                    high_part(half_v * 2 + par, half_v * 2 + (LONE + par), par)
            with act.Fori(0, LONE // 2) as half_b:
                high_part(half_b * 2 + (NB - LONE), half_b, 0)
                high_part(half_b * 2 + (NB - LONE + 1), half_b + LONE // 2, 1)

            def stationary(t, par):
                for dst, src in ((stat_h, zTh), (stat_l, zTl)):
                    ins = act.activation(dst[:, par, :], src[:, ds(t * P, P)].bitcast(F32), ACT.Copy)
                ins.then_inc(stat_ready, 1)

            def scores(t, par, last=False):
                for h in range(NH):
                    act.wait_ge(gram_ready, t * NH + h + 1)
                    q = h // 2
                    if h % 2 == 0:
                        act.wait_ge(quarter_free, t * NQ + q + 1)
                    ins = act.activation(keys[:, q, (h % 2) * HW:(h % 2 + 1) * HW],
                                         gb[:, 2 * (h % 2):2 * (h % 2) + 2, :].rearrange("p a b -> p (a b)"),
                                         ACT.Copy)
                    ins.then_inc(gram_free, 1) if h % 2 == 0 else ins.then_inc(quarter_ready, 1)
                    if h == 0 and not last:
                        stationary(t + 1, 1 - par)

            def load_group(g):
                if not isinstance(g, int) or g > 0:
                    act.wait_ge(yw_stored, 16 * g)
                act.dma_start(xw_g[:], xT[:, ds(g * (GT * P), GT * P)]).then_inc(xtg_loaded, 16)

            def load_x(g):
                act.dma_start(ystage[:], x_t[:, ds(g * GT, GT), :]).then_inc(xg_loaded, 16)

            def exp_group(g):
                act.wait_ge(v_ready, g + 1)
                act.activation(r_g[:].rearrange("p a b -> p (a b)"), v_g[:].rearrange("p a b -> p (a b)"),
                               ACT.Sqrt).then_inc(r_ready, 1)
                act.wait_ge(r_ready, g + 1)
                if not isinstance(g, int) or g > 0:
                    act.wait_ge(d2_ready, g)
                act.activation(s_g[:].rearrange("p a b -> p (a b)"), r_g[:].rearrange("p a b -> p (a b)"),
                               ACT.Exp, scale=-0.5).then_inc(s_ready, 1)

            def next_rows(g):
                act.wait_ge(ystage_ready, g + 1)
                act.wait_ge(prod_ready, (g * GT + 1) * IBS)
                act.activation(ycur[:], ystage[:].rearrange("p t f -> p (t f)"), ACT.Copy).then_inc(ycur_ready, 1)
                act.wait_ge(ycur_ready, g + 2)
                load_x(g + 1)

            def group(g, product, first=False, last=False):
                scores(g * GT, 0)
                scores(g * GT + 1, 1)
                if not first:
                    exp_group(g - 1)
                    load_group(g - 1)
                scores(g * GT + 2, 0)
                scores(g * GT + 3, 1)
                if product:
                    next_rows(g - 2)
                scores(g * GT + 4, 0)
                scores(g * GT + 5, 1)
                scores(g * GT + 6, 0)
                scores(g * GT + 7, 1, last=last)

            act.wait_ge(zl_done, NB)
            act.wait_ge(p2_rows, LONE)
            load_x(0)
            stationary(0, 0)
            group(0, False, first=True)
            group(1, False)
            with act.Fori(2, NG - 1) as g:
                group(g, True)
            group(NG - 1, True, last=True)
            act.wait_ge(gram_ready, NH * NT)
            act.dma_start(xt_last[:], xT[:, (NG - 1) * GT * P:NG * GT * P]).then_inc(xtg_loaded, 16)
            exp_group(NG - 1)
            next_rows(NG - 2)
            act.wait_ge(d2_ready, NG)
            act.wait_ge(xg_loaded, 16 * NG)
            act.wait_ge(prod_ready, ((NG - 1) * GT + 1) * IBS)
            for k in range(GT):
                ins = act.activation(ycur[:, k * D:(k + 1) * D], ystage[:, k, :], ACT.Copy, scale=d2_g[:, k:k + 1])
            ins.then_inc(ycur_ready, 1)

            def norm_load(q, par):
                act.dma_start(xb[:, par], x_t[:, ds(q * GT, GT), :]).then_inc(xb_loaded[par], 16)

            act.wait_ge(quarter_keyed, NQ * NT)
            act.wait_ge(pool_consts, CONSTS + 1)

            def finish(q, par, more):
                act.wait_ge(var_ready, q + 1)
                act.activation(sd[:], mv[:, :, 1], ACT.Sqrt, bias=eps_c[:]).then_inc(sd_ready, 1)
                act.wait_ge(y_ready, q + 1)
                act.dma_start(out_t[:, ds(q * GT, GT), :], y_out[:, par]).then_inc(y_stored[par], 16)
                if more:
                    norm_load(q + 2, par)

            act.dma_start(b2b[:], b2.partition_broadcast(P)).then_inc(b2_loaded, 16)
            norm_load(0, 0)
            norm_load(1, 1)
            with act.Fori(0, (GT - 2) // 2) as half_q:
                q = half_q * 2
                finish(q, 0, True)
                finish(q + 1, 1, True)
            finish(GT - 2, 0, False)
            finish(GT - 1, 1, False)
            for par in range(2):
                act.wait_ge(y_stored[par], 16 * (GT // 2 + 1))

        @block.tensor
        def _(pe):
            pe.wait_ge(pool_consts, CONSTS)

            for count in (z_ready, zt_ready):
                pe.sem_inc(count, 1)

            begun = set()
            for r, jb in pass1:
                if jb is None:
                    pe.wait_ge(acc_folded, 2 * (r + 1))
                    if r >= 1:
                        pe.wait_ge(y1_ready, r)
                    for it in range(TPB):
                        mm = pe.matmul(ps_rs[:, it:it + 1], acc[:, it * P:(it + 1) * P], ones[:, 0:1],
                                       start=True, stop=True)
                    mm.then_inc(rowsum_ready, 1)
                    continue
                slot, use = slot1(r, columns(r).index(jb))
                pe.wait_ge(loaded[slot], 16 * (use + 1))
                if r not in begun and r >= BANKS1:
                    pe.wait_ge(agg_saved, r - BANKS1 + 1)
                if jb >= r:
                    pe.wait_ge(y1_ready, jb + 1)
                for jt in range(TPB):
                    mm = pe.matmul(banks1[r % BANKS1], y1[:, (jb * TPB + jt) * D:(jb * TPB + jt + 1) * D],
                                   slots1[slot][:, jt * BLK:(jt + 1) * BLK],
                                   start=(r not in begun and jt == 0), stop=(jb == last_of[r] and jt == TPB - 1))
                begun.add(r)
                mm.then_inc(p1_rows if done1[r, jb][0] else p1_blocks, 1)

            def z_product(r):
                pe.wait_ge(usum_ready, r + 1)
                if r >= 1:
                    pe.wait_ge(z_done, r)
                for it in range(TPB):
                    mm = pe.matmul(ps_z[:, it * D:(it + 1) * D], usum[:, it * P:(it + 1) * P], w1[:],
                                   start=True, stop=True)
                mm.then_inc(z_ready, 1)

            def z_transpose(r):
                pe.wait_ge(z_done, r + 1)
                if r >= 1:
                    pe.wait_ge(zl_done, r)
                for it in range(TPB):
                    mm = pe.transpose(ps_zt[:, it * P:(it + 1) * P], z_c[:, it, :], ident[:])
                mm.then_inc(zt_ready, 1)

            def z_squares(r):
                pe.wait_ge(zsq_ready, r + 1)
                if r >= 2:
                    pe.wait_ge(sqb_done, r - 1)
                mm = pe.matmul(px[:, r % 2, :], ones[:], zsq[:], start=True, stop=True)
                mm.then_inc(sqb_ready, 1)

            FULL = NB - LONE
            pe.wait_ge(agg_saved, LONE)
            for m, (i, ib, jb) in enumerate(pass2):
                first = jb == ib + KEEP + 1
                if first and i >= 1:
                    pe.wait_ge(usum_ready, FULL + i - 1)
                pe.wait_ge(loaded[m % R2], 16 * (uses1(m % R2) + m // R2 + 1))
                for jt in range(TPB):
                    mm = pe.matmul(pp[:, 0, i % 2, :], y1[:, (jb * TPB + jt) * D:(jb * TPB + jt + 1) * D],
                                   ring2[:, m % R2, jt * BLK:(jt + 1) * BLK],
                                   start=(first and jt == 0), stop=(jb == NB - 1 and jt == TPB - 1))
                mm.then_inc(p2_rows if jb == NB - 1 else p2_blocks, 1)
                k = jb - (ib + KEEP + 1)
                if i == 0:
                    v, n = divmod(k, 3)
                    if n == 0:
                        z_product(v)
                    elif n == 1:
                        z_transpose(v)
                    else:
                        z_squares(v)
                else:
                    v = FULL + i - 1
                    most = NB - 1 - (ib + KEEP + 1)
                    if k == 0:
                        z_product(v)
                    if k == min(1, most):
                        z_transpose(v)
                    if k == min(2, most):
                        z_squares(v)
            z_product(NB - 1)
            z_transpose(NB - 1)
            z_squares(NB - 1)

            pe.wait_ge(zl_done, NB)
            pe.sem_inc(prod_ready, IBS)
            pe.sem_inc(block_used, IBS)

            def score_quarter(t, par, q):
                for h in range(2 * q, 2 * q + 2):
                    if h % 2 == 0:
                        pe.wait_ge(gram_free, t * NQ + q + 1)
                    else:
                        pe.wait_ge(quarter_ready, t * NQ + q + 1)
                    for c in range(2):
                        bank = gb[:, 2 * (h % 2) + c, :]
                        cols = slice((2 * h + c) * BLK, (2 * h + c + 1) * BLK)
                        pe.matmul(bank, stat_h[:, par, :], zTh[:, cols], start=True, stop=False)
                        pe.matmul(bank, stat_h[:, par, :], zTl[:, cols], start=False, stop=False)
                        mm = pe.matmul(bank, stat_l[:, par, :], zTh[:, cols], start=False, stop=True)
                    mm.then_inc(gram_ready, 1)

            def a_block(s, par, i, tail=False, last=False):
                c, b = divmod(i, BPG)
                if b == 0:
                    if last:
                        pe.wait_ge(ofin_ready, (s - (NG - 1) * GT - 2) * IBS + c + 1)
                    else:
                        pe.wait_ge(prod_free, s * IBS + c + 1)
                a = (a_tail if tail else a_ring)[:, i if tail else A_SLOTS[i], :]
                pe.wait_ge(a_loaded[i], (s + 1) * 16)
                for jt in range(TPB):
                    k = b * TPB + jt
                    mm = pe.matmul(pp[:, par, c, :], ycur[:, k * D:(k + 1) * D], a[:, jt * BLK:(jt + 1) * BLK],
                                   start=(k == 0), stop=(k == GT - 1))
                mm.then_inc(prod_ready if b == BPG - 1 else block_used, 1)

            def x_w2(g, banks, xt=xw_g):
                pe.wait_ge(xtg_loaded, 16 * (g + 1))
                for k in range(GT):
                    mm = pe.matmul(banks[:, k // TPB, (k % TPB) * D:(k % TPB + 1) * D], xt[:, k * P:(k + 1) * P],
                                   w2[:], start=True, stop=True)
                mm.then_inc(psx_ready, 1)

            def tile(g, k, par, ycur_count, table=False, after_table=False):
                t = g * GT + k
                product = ycur_count is not None
                pe.wait_ge(stat_ready, t + 1)
                for q in range(NQ):
                    if table and q == 2:
                        if product:
                            pe.wait_ge(prod_free, (t - LAG) * IBS + 2 * IBS)
                        x_w2(g - 1, px)
                    score_quarter(t, par, q)
                    if product:
                        if q == 0:
                            pe.wait_ge(ycur_ready, ycur_count)
                            if after_table:
                                pe.wait_ge(yw_done, g + 1)
                        a_block(t - LAG, par, q)

            def group(g, before, after, first=False):
                with pe.Fori(0, GT // 4) as half_k:
                    for par in range(2):
                        tile(g, half_k * 2 + par, par, before)
                tile(g, 4, 0, after)
                tile(g, 5, 1, after)
                tile(g, 6, 0, after, table=not first)
                tile(g, 7, 1, after, after_table=not first)

            assert IBS * BPG == NQ
            group(0, None, None, first=True)
            group(1, None, None)
            group(2, None, 2)
            with pe.Fori(3, NG) as g:
                group(g, g - 1, g)

            pe.wait_ge(quarter_ready, NQ * NT + 1)
            pe.wait_ge(gram_free, NQ * NT + 1)
            x_w2(NG - 1, gb[:, 2:4, :], xt_last)

            def tail_step(s, par, last=False):
                for i in range(IBS * BPG):
                    a_block(s, par, i, tail=True, last=last)

            def tail_group(g, q0):
                pe.wait_ge(ycur_ready, g + 2)
                with pe.Fori(q0 // 2, GT // 2) as half_k:
                    for par in range(2):
                        tail_step(half_k * 2 + (g * GT + par), par)

            tail_group(MID // GT, MID % GT)
            tail_group(NG - 2, 0)

            def last_product(q, par):
                pe.wait_ge(ofin_ready, IBS * (q + 1))
                pe.wait_ge(fin_step, q + 1)
                for c in range(IBS):
                    for it in range(TPB):
                        mm = pe.matmul(gb[:, 2 * par + c, it * D:(it + 1) * D],
                                       ofin[:, par, c, it * P:(it + 1) * P], w2[:], start=True, stop=True)
                mm.then_inc(fin_ready, 1)

            def last_step(q, par, last):
                for i in range(IBS * BPG):
                    if i == BPG and (last or par):
                        last_product(q - 1, 1 - par)
                    a_block(q + (NG - 1) * GT, par, i, tail=True, last=last)

            pe.wait_ge(ycur_ready, NG + 1)
            last_step(0, 0, False)
            last_step(1, 1, False)
            with pe.Fori(1, GT // 2) as half_q:
                for par in range(2):
                    last_step(half_q * 2 + par, par, True)
            last_product(GT - 1, 1)

        @block.vector
        def _(dve):
            dve.sem_inc(yw_done, 1)

            for r in range(NB):
                before, _ = slot1(r, 0)
                for k in range(1, NB):
                    slot, use = slot1(r, k)
                    if k == 1:
                        dve.wait_ge(loaded[before], (slot1(r, 0)[1] + 1) * 16)
                        if r:
                            dve.wait_ge(rowsum_ready, r)
                    else:
                        dve.wait_ge(rows_added, r * (NB - 1) + k - 1)
                    dve.wait_ge(loaded[slot], (use + 1) * 16)
                    dve.tensor_tensor(acc[:], slots1[before] if k == 1 else acc[:], slots1[slot],
                                      ALU.add).then_inc(rows_added, 1)
                for n in (2, 1):
                    if n == 2:
                        dve.wait_ge(rows_added, (r + 1) * (NB - 1))
                    else:
                        dve.wait_ge(acc_folded, 2 * r + 1)
                    dve.tensor_tensor(acc[:, 0:n * BLK], acc[:, 0:n * BLK], acc[:, n * BLK:2 * n * BLK],
                                      ALU.add).then_inc(acc_folded, 1)

            dve.wait_ge(p1_rows, NB)
            dve.wait_ge(consts_loaded, 4 * 16)

            def finish_z(v, ib):
                at = 7 * v
                dve.tensor_copy(d1_z[:], d1_all[:, ds(ib * TPB, TPB)]).then_inc(zstep, 1)
                dve.wait_ge(zstep, at + 1)
                dve.wait_ge(z_ready, v + 2)
                dve.wait_ge(zt_ready, v + 1)
                for it in range(TPB):
                    dve.scalar_tensor_tensor(out=z_c[:, it, :], in0=ps_z[:, it * D:(it + 1) * D],
                                             scalar=d1_z[:, it:it + 1], in1=b1b[:], op0=ALU.mult,
                                             op1=ALU.add).then_inc(zstep, 1)
                zf = z_c[:].rearrange("p a b -> p (a b)")
                dve.wait_ge(zstep, at + 5)
                dve.scalar_tensor_tensor(out=zf, in0=zf, scalar=0.1, in1=zf, op0=ALU.mult,
                                         op1=ALU.max).then_inc(zstep, 1)
                dve.wait_ge(zstep, at + 6)
                for it in range(TPB):
                    ins = dve.tensor_tensor_reduce(out=junk[:, it, :], in0=z_c[:, it, :], in1=z_c[:, it, :],
                                                   scale=1.0, scalar=0.0, op0=ALU.mult, op1=ALU.add,
                                                   accum_out=sq_c[:, it:it + 1])
                ins.then_inc(zstep, 1)
                dve.wait_ge(zstep, at + 7)
                dve.tensor_copy(sq_all[:, ds(ib * TPB, TPB)], sq_c[:]).then_inc(z_done, 1)
                dve.wait_ge(zh_done, v + 1)
                cols = ds(ib * BLK, BLK)
                dve.tensor_tensor(zTl[:, cols], ps_zt, zTh[:, cols].bitcast(F32),
                                  ALU.subtract).then_inc(zl_done, 1)

            for ib in range(LONE, NB):
                v = ib - LONE
                dve.wait_ge(z_ready, v + 1)
                dve.tensor_copy(usum[:], banks1[ib % BANKS1]).then_inc(usum_ready, 1)
                finish_z(v, ib)

            def row2(i, ib, par):
                dve.wait_ge(p2_rows, i + 1)
                dve.wait_ge(z_ready, i + (NB - LONE + 1))
                dve.tensor_tensor(usum[:], pp[:, 0, par, :], aggT[:, ds(ib * BLK, BLK)],
                                  ALU.add).then_inc(usum_ready, 1)
                finish_z(i + (NB - LONE), ib)

            dve.wait_ge(agg_saved, LONE)
            with dve.Fori(0, LONE // 2) as half_i:
                row2(half_i * 2, half_i, 0)
                row2(half_i * 2 + 1, half_i + LONE // 2, 1)

            dve.sem_inc(quarter_free, NQ)
            dve.sem_inc(prod_free, 2 * IBS)

            def table_rows(g, banks):
                dve.wait_ge(psx_ready, g + 1)
                dve.wait_ge(d2_ready, g + 1)
                if not isinstance(g, int) or g > 0:
                    dve.wait_ge(yw_stored, 16 * g)
                for c in range(2):
                    ins = dve.tensor_tensor(
                        xw_g[:, c * BLK:(c + 1) * BLK].rearrange("p (t f) -> p t f", f=D),
                        banks[:, c, :].rearrange("p (t f) -> p t f", f=D),
                        d2_g[:, c * TPB:(c + 1) * TPB].unsqueeze(2).to_broadcast([P, TPB, D]), ALU.mult)
                ins.then_inc(yw_done, 1)

            def place_to_row(g, n):
                dve.wait_ge(grp_step, g * 16 + 3 + n)
                if n == 0:
                    dve.tensor_tensor(cand_f[:], cand_f[:], quarter_at[:].unsqueeze(1).to_broadcast([P, GT, NC]),
                                      ALU.add).then_inc(grp_step, 1)
                elif n == 3 * KNN + 1:
                    dve.tensor_copy(nb_all[:, ds(g * (GT * KNN), GT * KNN)],
                                    nb_f[:].rearrange("p a b -> p (a b)")).then_inc(nb_ready, 1)
                else:
                    k, part = divmod(n - 1, 3)
                    if part == 0:
                        dve.tensor_tensor(pick[:], iota_c[:].unsqueeze(1).to_broadcast([P, GT, NC]),
                                          top_f[:, :, k:k + 1].to_broadcast([P, GT, NC]), ALU.is_equal
                                          ).then_inc(grp_step, 1)
                    elif part == 1:
                        dve.tensor_tensor(pick[:], pick[:], cand_f[:], ALU.mult).then_inc(grp_step, 1)
                    else:
                        dve.tensor_reduce(nb_f[:, :, k], pick[:], AX_X, ALU.add).then_inc(grp_step, 1)

            ROW_STEPS = 3 * KNN + 2

            def neighbours(g, k, table, first):
                at = (g * GT + k) * (NQ + 1)
                all8 = cand[:, k % 2, :]

                def largest(q):
                    dve.wait_ge(quarter_keyed, (g * GT + k) * NQ + q + 1)
                    apart(dve)
                    dve.max(cand[:, k % 2, q * TOP:(q + 1) * TOP], keys[:, q, :]).then_inc(knn_step, 1)

                def places(q):
                    dve.wait_ge(knn_step, at + q + 1)
                    apart(dve)
                    dve.max_index(cand_at[:, k, q * TOP:(q + 1) * TOP], cand[:, k % 2, q * TOP:(q + 1) * TOP],
                                  keys[:, q, :]).then_inc(quarter_free, 1)

                for q in range(NQ - 1):
                    largest(q)
                    n = k * (NQ - 1) + q
                    if not first and n < ROW_STEPS:
                        place_to_row(g - 1, n)
                    places(q)
                if table:
                    table_rows(g - 1, px)
                largest(NQ - 1)
                dve.wait_ge(knn_step, at + NQ)
                apart(dve)
                dve.max(topv[:, k, :], all8).then_inc(knn_step, 1)
                places(NQ - 1)
                dve.wait_ge(knn_step, at + NQ + 1)
                apart(dve)
                dve.max_index(top_at[:, k, :], topv[:, k, :], all8).then_inc(top_ready, 1)

            def add_product(s, q, c, par):
                dve.wait_ge(prod_ready, s * IBS + c + 1 + IBS)
                cols = q * IBS * BLK + c * BLK
                cols = ds(cols, BLK) if not isinstance(cols, int) else slice(cols, cols + BLK)
                dve.tensor_tensor(aggT[:, cols], aggT[:, cols], pp[:, par, c, :], ALU.add).then_inc(prod_free, 1)

            def distances(g):
                at = g * 16
                if not isinstance(g, int) or g > 0:
                    dve.wait_ge(r_ready, g)
                dve.wait_ge(top_ready, g * GT + GT)
                sq = sq_all[:, ds(g * GT, GT)].unsqueeze(2).to_broadcast([P, GT, KNN])
                dve.scalar_tensor_tensor(out=v_g[:], in0=topv[:, :, 0:KNN], scalar=-2.0, in1=sq,
                                         op0=ALU.mult, op1=ALU.add).then_inc(grp_step, 1)
                dve.wait_ge(grp_step, at + 1)
                dve.tensor_scalar(v_g[:], v_g[:], 0.0, EPS_D2, ALU.max, ALU.add).then_inc(v_ready, 1)
                dve.tensor_copy(top_f[:], top_at[:, :, 0:KNN]).then_inc(grp_step, 1)
                dve.tensor_copy(cand_f[:], cand_at[:]).then_inc(grp_step, 1)

            def group(g, halves, first=False):
                for k in range(GT):
                    neighbours(g, k, k == GT - 2 and not first, first)
                    if halves[k // (GT // 2)]:
                        for c in range(IBS):
                            add_product(g * GT + (k - LAG), (k - LAG) % GT, c, k % 2)
                distances(g)

            dve.wait_ge(pool_consts, CONSTS)
            group(0, (False, False), first=True)
            dve.wait_ge(agg_zeroed, 1)
            group(1, (False, False))
            group(2, (False, True))
            with dve.Fori(3, NG) as g:
                group(g, (True, True))

            for n in range(ROW_STEPS):
                place_to_row(NG - 1, n)

            dve.wait_ge(gram_ready, NH * NT)
            dve.sem_inc(gsum_done, 2)

            def sum_neighbours(s, par):
                dve.tensor_copy(s_c[:, par, :], s_all[:, ds(s * (4 * KNN), 4 * KNN)]).then_inc(scal_ready, 1)
                dve.wait_ge(scal_ready, s + 1)
                dve.wait_ge(gathered[par], (s - par) * (4 * KNN * 8) + 16 * 4 * KNN)
                for k in range(KNN):
                    if k:
                        dve.wait_ge(gs_step, s * 3 + k)
                    for i in range(4):
                        to = gsum[:, ds(s * (4 * D) + i * D, D)]
                        j = i * KNN + k
                        if k == 0:
                            ins = dve.tensor_scalar(to, rows4[:, par, j, :], s_c[:, par, j:j + 1], None, ALU.mult)
                        else:
                            ins = dve.scalar_tensor_tensor(out=to, in0=rows4[:, par, j, :],
                                                           scalar=s_c[:, par, j:j + 1], in1=to,
                                                           op0=ALU.mult, op1=ALU.add)
                    ins.then_inc(gsum_done if k == KNN - 1 else gs_step, 1)

            def step(s, par):
                for c in range(IBS):
                    add_product(s, s % GT if isinstance(s, int) else s - (NG - 2) * GT, c, par)

            table_rows(NG - 1, gb[:, 2:4, :])
            dve.wait_ge(yw_done, NG + 1)
            dve.sem_inc(fin_step, 2)
            for s in range(MID, MID + 3):
                step(s, s % 2)
            sum_neighbours(0, 0)
            step(MID + 3, 1)
            with dve.Fori(0, 3) as half_q:
                for par in range(2):
                    sum_neighbours(half_q * 2 + (1 + par), 1 - par)
                    step(half_q * 2 + ((NG - 2) * GT + par), par)
            sum_neighbours(GT - 1, 1)
            step((NG - 1) * GT - 2, 0)
            step((NG - 1) * GT - 1, 1)

            def complete(q, par, c):
                dve.wait_ge(prod_ready, (q + (NG - 1) * GT) * IBS + c + 1 + IBS)
                dve.tensor_tensor(ofin[:, par, c, :], aggT[:, ds(q * (IBS * BLK) + c * BLK, BLK)],
                                  pp[:, par, c, :], ALU.add).then_inc(ofin_ready, 1)

            def norm(q, par):
                at = q * 5
                dve.wait_ge(fin_ready, q + 1)
                dve.wait_ge(gsum_done, 2 * q + 4)
                if not isinstance(q, int) or q > 0:
                    dve.wait_ge(y_ready, q)
                for c in range(IBS):
                    ins = dve.tensor_tensor(res[:, c * TPB:(c + 1) * TPB, :].rearrange("p t f -> p (t f)"),
                                            gb[:, 2 * par + c, :], gsum[:, ds(q * (GT * D) + c * BLK, BLK)], ALU.add)
                ins.then_inc(fin_step, 1)
                dve.tensor_copy(d2_f[:], d2_all[:, ds(q * GT, GT)]).then_inc(norm_step, 1)
                if isinstance(q, int) and q == 0:
                    dve.wait_ge(b2_loaded, 16)
                dve.wait_ge(xb_loaded[par], (q - par) * 8 + 16)
                dve.tensor_tensor(xb[:, par], xb[:, par], b2b[:].unsqueeze(1).to_broadcast([P, GT, D]),
                                  ALU.add).then_inc(norm_step, 1)
                dve.wait_ge(fin_step, q + 3)
                dve.wait_ge(norm_step, at + 2)
                for i in range(GT):
                    ins = dve.scalar_tensor_tensor(out=res[:, i, :], in0=res[:, i, :], scalar=d2_f[:, i:i + 1],
                                                   in1=xb[:, par, i, :], op0=ALU.mult, op1=ALU.add)
                ins.then_inc(norm_step, 1)
                dve.wait_ge(norm_step, at + 3)
                for i in range(GT):
                    ins = dve.bn_stats(stats[:, i, :], res[:, i, :])
                ins.then_inc(norm_step, 1)
                dve.wait_ge(norm_step, at + 4)
                apart(dve)
                for i in range(GT):
                    ins = dve.bn_aggr(mv[:, i, :], stats[:, i, :])
                ins.then_inc(var_ready, 1)
                dve.wait_ge(sd_ready, q + 1)
                dve.reciprocal(rstd[:], sd[:]).then_inc(norm_step, 1)
                dve.wait_ge(norm_step, at + 5)
                dve.wait_ge(y_stored[par], (q - par) * 8 + 16)
                for i in range(GT):
                    ins = dve.tensor_scalar(y_out[:, par, i, :], res[:, i, :], mv[:, i, 0:1], rstd[:, i:i + 1],
                                            ALU.subtract, ALU.mult)
                ins.then_inc(y_ready, 1)

            complete(0, 0, 0)
            complete(0, 0, 1)
            sum_neighbours(GT, 0)
            complete(1, 1, 0)
            norm(0, 0)
            complete(1, 1, 1)
            sum_neighbours(GT + 1, 1)
            with dve.Fori(1, GT // 2) as half_q:
                q = half_q * 2
                for par in range(2):
                    complete(q + par, par, 0)
                    norm(q + (par - 1), 1 - par)
                    complete(q + par, par, 1)
                    sum_neighbours(q + (GT + par), par)
            norm(GT - 1, 1)


def kernel(x, adj, L0_gnn_W1, L0_gnn_b1, L0_gnn_W2, L0_gnn_b2):
    import numpy as np
    import concourse.bacc as bacc
    from concourse.bass_utils import run_bass_kernel_spmd

    x, adj = np.asarray(x), np.asarray(adj)
    nb = adj.shape[0] // BLK
    arrays = {
        "x": np.ascontiguousarray(x),
        "xT": np.ascontiguousarray(x.T),
        "adjb": np.ascontiguousarray(
            adj.reshape(nb, BLK, nb, TPB, P).transpose(0, 2, 4, 3, 1)).reshape(nb, nb, P, TPB * BLK),
        "W1": np.ascontiguousarray(L0_gnn_W1), "b1": np.ascontiguousarray(L0_gnn_b1),
        "W2": np.ascontiguousarray(L0_gnn_W2), "b2": np.ascontiguousarray(L0_gnn_b2),
    }
    nc = bacc.Bacc("TRN2", target_bir_lowering=False, num_devices=1)
    args = {n: nc.dram_tensor(n, a.shape, mybir.dt.from_np(a.dtype), kind="ExternalInput").ap()
            for n, a in arrays.items()}
    args["out"] = nc.dram_tensor("out", x.shape, F32, kind="ExternalOutput").ap()
    gnn_resnorm(nc, **args)
    r = run_bass_kernel_spmd(nc, [arrays], core_ids=[0])
    return r.results[0]["out"]
```
